# Optimizing a Trainium2 kernel written in Bass

```python
import numpy as np
import jax
import jax.numpy as jnp

def _softmax(x, axis=-1):
    return jax.nn.softmax(x, axis=axis)

def _gelu(x):
    return jax.nn.gelu(x, approximate=True)

def _silu(x):
    return jax.nn.silu(x)

def _sigmoid(x):
    return jax.nn.sigmoid(x)

def _layernorm(x, axis=-1, eps=1e-05):
    m = jnp.mean(x, axis=axis, keepdims=True)
    v = jnp.var(x, axis=axis, keepdims=True)
    return (x - m) / jnp.sqrt(v + eps)

def _scatter_add(tgt, idx, src, axis=0):
    return tgt.at[idx].add(src)

def _segment_sum(src, seg, n):
    return jax.ops.segment_sum(src, seg, n)
kernel_name = 'mk_flamingo_gated_d1_seqx_r2_bb7289'

def setup_inputs(seed: int=0):
    np.random.seed(seed)
    _w = jnp.asarray

    def _rec_inputs():
        import jax
        import jax.numpy as jnp
        _rk = jax.random.key(seed)
        x = -0.000125 + 0.9999 * jax.random.normal(jax.random.fold_in(_rk, 1), (8, 512, 2048), jnp.float32)
        _lenS = 512 - jax.random.randint(jax.random.fold_in(_rk, 7), (8,), 0, max(1, 512 // 4) + 1, jnp.int32)
        _lenS2 = 512 - jax.random.randint(jax.random.fold_in(_rk, 8), (8,), 0, max(1, 512 // 4) + 1, jnp.int32)
        _ctx_4096P = jax.random.normal(jax.random.fold_in(_rk, 11), (8, 16, 2048), jnp.float32)
        _ctx_4096c = jax.random.dirichlet(jax.random.fold_in(_rk, 511), 0.3 * jnp.ones((16,), jnp.float32), (8, 512))
        _ctx_4096t = jnp.einsum('bsk,bkd->bsd', _ctx_4096c, _ctx_4096P)
        _ctx_4096t = _ctx_4096t * jax.lax.rsqrt(jnp.mean(jnp.square(_ctx_4096t)) + 1e-12) * 0.953939
        ctx_4096 = -1.52775e-05 + 0.999936 * (_ctx_4096t + 0.3 * jax.random.normal(jax.random.fold_in(_rk, 611), (8, 512, 2048), jnp.float32))
        _g = jax.random.normal(jax.random.fold_in(_rk, 9001), (2, 1), jnp.float32)
        _g = jnp.sign(_g) * jnp.maximum(jnp.abs(_g), 1.0) + (_g == 0) * 1.0
        g_xattn = _g[0]
        g_ffn = _g[1]
        return (x, ctx_4096, g_xattn, g_ffn)
    x, ctx_4096, g_xattn, g_ffn = _rec_inputs()

    def _L0_xattn_setup():
        import jax, jax.numpy as jnp
        import numpy as np
        H = 8
        C = 2

        def _autocorrelation(Q, K, V):
            B, L, D = Q.shape
            d = D // H
            q = Q.reshape(B, L, H, d).transpose(0, 2, 1, 3)
            k = K.reshape(B, L, H, d).transpose(0, 2, 1, 3)
            v = V.reshape(B, L, H, d).transpose(0, 2, 1, 3)
            qf = jnp.fft.fft(q, axis=2)
            kf = jnp.fft.fft(k, axis=2)
            corr = jnp.fft.ifft(qf * jnp.conj(kf), axis=2).real
            topk = int(C * np.log(L))
            w, idx = jax.lax.top_k(corr.transpose(0, 1, 3, 2), topk)
            w = jax.nn.softmax(w, axis=-1)
            pos = jnp.arange(L)[:, None]
            out = jnp.zeros_like(v)
            for i in range(topk):
                g = jnp.minimum(idx[:, :, None, :, i] + pos, L - 1)
                out = out + w[:, :, None, :, i] * jnp.take_along_axis(v, g, axis=2)
            return out.transpose(0, 2, 1, 3).reshape(B, L, D)
        key = jax.random.key(seed)
        k1, k2, k3 = jax.random.split(key, 3)
        B, L, D = (16, 256, 2048)
        Q = jax.random.normal(k1, (B, L, D), dtype=jnp.float32)
        K = jax.random.normal(k2, (B, L, D), dtype=jnp.float32)
        V = jax.random.normal(k3, (B, L, D), dtype=jnp.float32)
        return {'Q': Q, 'K': K, 'V': V}
    _L0_xattn_all = _L0_xattn_setup()
    _L0_xattn_in = {k: v for k, v in _L0_xattn_all.items() if k in ()}
    del _L0_xattn_all

    def _L0_ffn_setup():
        import jax, jax.numpy as jnp
        import numpy as np
        B, S, D, O, E, R = (4, 1024, 2048, 2048, 8, 16)
        SCALING = 32.0 / 16.0
        MAX_THRESHOLD = 0.125
        key = jax.random.key(seed)
        ks = jax.random.split(key, 8)
        return {'x': jax.random.normal(ks[0], (B, S, D), jnp.float32), 'W_base': jax.random.normal(ks[1], (O, D), jnp.float32) * (1.0 / np.sqrt(D)), 'b_base': jax.random.normal(ks[2], (O,), jnp.float32) * 0.02, 'W_gate': jax.random.normal(ks[3], (E, D), jnp.float32) * (1.0 / np.sqrt(D)), 'W_thr': jax.random.normal(ks[4], (D,), jnp.float32) * (1.0 / np.sqrt(D)), 'b_thr': jax.random.normal(ks[5], (1,), jnp.float32) * 0.02, 'A_w': jax.random.normal(ks[6], (E, R, D), jnp.float32) * (1.0 / np.sqrt(D)), 'B_w': jax.random.normal(ks[7], (E, O, R), jnp.float32) * (1.0 / np.sqrt(R))}
    _L0_ffn_all = _L0_ffn_setup()
    _L0_ffn_in = {k: v for k, v in _L0_ffn_all.items() if k in ('W_base', 'b_base', 'W_gate', 'W_thr', 'b_thr', 'A_w', 'B_w')}
    del _L0_ffn_all
    return {'x': x, 'ctx_4096': ctx_4096, 'g_xattn': g_xattn, 'g_ffn': g_ffn, 'L0_ffn_W_base': _L0_ffn_in['W_base'], 'L0_ffn_b_base': _L0_ffn_in['b_base'], 'L0_ffn_W_gate': _L0_ffn_in['W_gate'], 'L0_ffn_W_thr': _L0_ffn_in['W_thr'], 'L0_ffn_b_thr': _L0_ffn_in['b_thr'], 'L0_ffn_A_w': _L0_ffn_in['A_w'], 'L0_ffn_B_w': _L0_ffn_in['B_w']}

def reference(x, ctx_4096, g_xattn, g_ffn, L0_ffn_W_base, L0_ffn_b_base, L0_ffn_W_gate, L0_ffn_W_thr, L0_ffn_b_thr, L0_ffn_A_w, L0_ffn_B_w):
    import jax
    import jax.numpy as jnp

    def _L0_xattn_ref(Q, K, V):
        import jax, jax.numpy as jnp
        import numpy as np
        H = 8
        C = 2

        def _autocorrelation(Q, K, V):
            B, L, D = Q.shape
            d = D // H
            q = Q.reshape(B, L, H, d).transpose(0, 2, 1, 3)
            k = K.reshape(B, L, H, d).transpose(0, 2, 1, 3)
            v = V.reshape(B, L, H, d).transpose(0, 2, 1, 3)
            qf = jnp.fft.fft(q, axis=2)
            kf = jnp.fft.fft(k, axis=2)
            corr = jnp.fft.ifft(qf * jnp.conj(kf), axis=2).real
            topk = int(C * np.log(L))
            w, idx = jax.lax.top_k(corr.transpose(0, 1, 3, 2), topk)
            w = jax.nn.softmax(w, axis=-1)
            pos = jnp.arange(L)[:, None]
            out = jnp.zeros_like(v)
            for i in range(topk):
                g = jnp.minimum(idx[:, :, None, :, i] + pos, L - 1)
                out = out + w[:, :, None, :, i] * jnp.take_along_axis(v, g, axis=2)
            return out.transpose(0, 2, 1, 3).reshape(B, L, D)
        return _autocorrelation(Q, K, V)

    def _L0_ffn_ref(x, W_base, b_base, W_gate, W_thr, b_thr, A_w, B_w):
        import jax, jax.numpy as jnp
        import numpy as np
        B, S, D, O, E, R = (4, 1024, 2048, 2048, 8, 16)
        SCALING = 32.0 / 16.0
        MAX_THRESHOLD = 0.125
        base = jnp.einsum('bsd,od->bso', x, W_base) + b_base
        xf = x.reshape(-1, D)
        gate = jax.nn.softmax(xf @ W_gate.T, axis=-1)
        thr = jax.nn.sigmoid(xf @ W_thr + b_thr[0]) * MAX_THRESHOLD
        adapted = gate - thr[:, None]
        selected = (adapted >= 0).astype(x.dtype)
        w = adapted * selected
        wsum = jnp.sum(w, axis=-1, keepdims=True)
        wsum = jnp.where(wsum == 0, jnp.ones_like(wsum), wsum)
        w = w / wsum
        h = jnp.einsum('nd,erd->ner', xf, A_w)
        moe = jnp.einsum('ner,ne,eor->no', h, w, B_w) * SCALING
        return base + moe.reshape(base.shape)
    x = x + jnp.tanh(g_xattn[0]) * _L0_xattn_ref(_layernorm(x, axis=-1), ctx_4096, ctx_4096)
    x = x + jnp.tanh(g_ffn[0]) * _L0_ffn_ref(_layernorm(x, axis=-1), L0_ffn_W_base, L0_ffn_b_base, L0_ffn_W_gate, L0_ffn_W_thr, L0_ffn_b_thr, L0_ffn_A_w, L0_ffn_B_w)
    return x

_drawn_inputs = setup_inputs


def setup_inputs(seed=0):
    import zlib

    import numpy as np

    out = dict(_drawn_inputs(seed))
    spreads = {}
    factors = {'L0_ffn_b_base': 5.933}
    for name, (base, spread) in spreads.items():
        noise = np.random.default_rng([zlib.crc32(name.encode()), seed]).standard_normal(out[name].shape)
        drawn = base * np.exp(spread * noise) if base else spread * noise
        out[name] = jnp.asarray(drawn.astype(out[name].dtype))
    for name, factor in factors.items():
        out[name] = (out[name] * factor).astype(out[name].dtype)
    return out
```

```python
import concourse.bass as bass
from concourse import mybir
from contextlib import ExitStack
import numpy as np

B, L, D = 8, 512, 2048
C = 512
HALF = L // 2
TT = L // 128
NCH = D // C
STEPS = B * NCH
CT = C // 128
TOPK = int(2 * np.log(L))
EPS = 1e-5
ROWS = B * L // 128
E, R = 8, 16
KD = D // 128
NG = E * R + E + 1
SCALING = 2.0
MAX_THRESHOLD = 0.125
N_SCALE, W_SCALE = 16.0, 64.0

ER, EI, EIZ, ERZM, ERZP, OR, OI = range(7)
FWD = 7 * 2 * 128
INV = 4 * HALF
TABLE = FWD + INV + 128


def dft_tables():
    t = np.arange(HALF)[:, None].astype(np.float64)
    g = np.arange(128)[None, :].astype(np.float64)
    even, odd = 2 * np.pi * g * t / HALF, 2 * np.pi * (2 * g + 1) * t / L
    nyquist = np.cos(np.pi * t[:, 0])
    er, eiz, o_r, oi = np.cos(even), -np.sin(even), np.cos(odd), -np.sin(odd)
    ei, erzm, erzp = eiz.copy(), er.copy(), er.copy()
    ei[:, 0], erzm[:, 0], erzp[:, 0] = nyquist, -nyquist, nyquist
    fwd = np.stack([er, ei, eiz, erzm, erzp, o_r, oi])
    fwd = fwd.reshape(7, 2, 128, 128).transpose(2, 0, 1, 3).reshape(128, FWD)
    ier, iei, ior, ioi = 2 * er.T / L, 2 * eiz.T / L, 2 * o_r.T / L, 2 * oi.T / L
    ier[0] /= 2
    iei[0] = nyquist / L
    inv = np.stack([ier, ior, iei, ioi], axis=1).reshape(128, INV)
    return np.concatenate([fwd, inv, np.eye(128)], axis=1).astype(np.float32)




def newton(dve, step, done, sqrt_done, sqrt_n, var, std, tmp, mean, scale, bias, factor):
    ALU = mybir.AluOpType
    dve.wait_ge(sqrt_done, sqrt_n)
    dve.reciprocal(scale[:, :], std[:, :]).then_inc(step, 1)
    dve.wait_ge(step, done + 1)
    dve.tensor_tensor(tmp[:, :], scale[:, :], scale[:, :], ALU.mult).then_inc(step, 1)
    dve.wait_ge(step, done + 2)
    dve.tensor_tensor(tmp[:, :], tmp[:, :], var[:, :], ALU.mult).then_inc(step, 1)
    dve.wait_ge(step, done + 3)
    dve.tensor_scalar(tmp[:, :], tmp[:, :], -0.5 * factor, 1.5 * factor, ALU.mult, ALU.add).then_inc(step, 1)
    dve.wait_ge(step, done + 4)
    dve.tensor_tensor(scale[:, :], scale[:, :], tmp[:, :], ALU.mult).then_inc(step, 1)
    dve.wait_ge(step, done + 5)
    dve.scalar_tensor_tensor(out=bias[:, :], in0=mean, scalar=-1.0, in1=scale[:, :],
                             op0=ALU.mult, op1=ALU.mult).then_inc(step, 1)


def flamingo_kernel(nc, x, ctx_v, g_xattn, g_ffn, w_base, b_base, w_gate, w_thr, b_thr, a_w, b_w,
                    tables, out):
    f32, f16 = mybir.dt.float32, mybir.dt.float16
    ALU, ACT, AX = mybir.AluOpType, mybir.ActivationFunctionType, mybir.AxisListType
    ds = bass.ds

    x2 = nc.dram_tensor("x2_scratch", (B, L, D), f32, kind="Internal").ap()
    x_t = x.rearrange("b (k p) c -> b p k c", p=128)
    v_t = ctx_v.rearrange("b (k p) c -> b p k c", p=128)
    x2_t = x2.rearrange("b (k p) c -> b p k c", p=128)
    x_rows = x.rearrange("b (k p) c -> (b k) p c", p=128)
    x2_rows = x2.rearrange("b (k p) c -> (b k) p c", p=128)
    out_rows = out.rearrange("b (k p) c -> (b k) p c", p=128)

    whole = ExitStack()
    with whole:
        def sem(name):
            return whole.enter_context(nc.semaphore(name))

        def keep(name, shape, dt=f32):
            return whole.enter_context(nc.sbuf_tensor(name, shape, dt))

        ident = keep("ident", [128, 128])
        ln1_scale, ln1_bias = keep("ln1_scale", [128, ROWS]), keep("ln1_bias", [128, ROWS])
        x2_stats = keep("x2_stats", [128, ROWS, NCH, 6])
        gates = keep("gates", [128, 2])
        bank = [whole.enter_context(nc.psum_tensor(f"bank{n}", [128, 512], f32)) for n in range(8)]

        ident_loaded, gates_loaded, gates_ready = sem("ident_loaded"), sem("gates_loaded"), sem("gates_ready")

        NB0 = 4
        with ExitStack() as s:
            xrow = s.enter_context(nc.sbuf_tensor("xrow", [128, NB0, D], f32))
            stats = s.enter_context(nc.sbuf_tensor("stats", [128, ROWS, NCH, 6], f32))
            mv = s.enter_context(nc.sbuf_tensor("mv", [128, ROWS, 2], f32))
            var, std, tmp = (s.enter_context(nc.sbuf_tensor(n, [128, ROWS], f32)) for n in ("var", "std", "tmp"))
            row_loaded = [sem(f"row_loaded{n}") for n in range(NB0)]
            row_used, ln1_step, ln1_sqrt = sem("row_used"), sem("ln1_step"), sem("ln1_sqrt")
            block = s.enter_context(nc.Block())

            @block.sync
            def _(sp):
                sp.dma_start(ident[:, :], tables[:, FWD + INV:TABLE]).then_inc(ident_loaded, 16)
                sp.dma_start(gates[:, 0:1], g_xattn.to_broadcast([128, 1])).then_inc(gates_loaded, 16)
                sp.dma_start(gates[:, 1:2], g_ffn.to_broadcast([128, 1])).then_inc(gates_loaded, 16)
                for n in range(NB0):
                    sp.dma_start(xrow[:, n, :], x_rows[n]).then_inc(row_loaded[n], 16)
                with sp.Fori(1, ROWS // NB0) as m:
                    for n in range(NB0):
                        sp.wait_ge(row_used, (m - 1) * NB0 + n + 1)
                        sp.nop(nofuse=True)
                        sp.dma_start(xrow[:, n, :], x_rows[m * NB0 + n]).then_inc(row_loaded[n], 16)

            @block.scalar
            def _(act):
                act.wait_ge(gates_loaded, 32)
                act.activation(gates[:, :], gates[:, :], ACT.Tanh).then_inc(gates_ready, 1)
                act.wait_ge(ln1_step, 1)
                act.activation(std[:, :], var[:, :], ACT.Sqrt).then_inc(ln1_sqrt, 1)

            @block.vector
            def _(dve):
                with dve.Fori(0, ROWS // NB0) as m:
                    for n in range(NB0):
                        dve.wait_ge(row_loaded[n], 16 * (m + 1))
                        for q in range(NCH):
                            op = dve.bn_stats(stats[:, m * NB0 + n, q, :], xrow[:, n, q * C:(q + 1) * C])
                        op.then_inc(row_used, 1)
                dve.wait_ge(row_used, ROWS)
                for r in range(ROWS):
                    op = dve.bn_aggr(mv[:, r, :], stats[:, r, :, :].rearrange("p a b -> p (a b)"))
                op.then_inc(row_used, 1)
                dve.wait_ge(row_used, ROWS + 1)
                dve.tensor_scalar(var[:, :], mv[:, :, 1], EPS, None, ALU.add).then_inc(ln1_step, 1)
                newton(dve, ln1_step, 1, ln1_sqrt, 1, var, std, tmp, mv[:, :, 0], ln1_scale, ln1_bias, 1.0)

        with ExitStack() as s:
            def sb(name, shape, dt=f32):
                return s.enter_context(nc.sbuf_tensor(name, shape, dt))

            table = sb("table", [128, FWD + INV])
            fwd = table[:, 0:FWD].rearrange("p (a j g) -> p a j g", a=7, j=2)
            inv = table[:, FWD:FWD + INV].rearrange("p (a q) -> p a q", a=4)
            xt = sb("xt", [128, 2, TT, C])
            qf = sb("qf", [128, TT, C])
            vt = sb("vt", [128, 2, TT, C])
            v_last = sb("v_last", [128, 2, C])
            kf = sb("kf", [128, TT, C])
            spec_v1 = sb("spec_v1", [128, 2, 4, C])
            spec_v = sb("spec_v", [128, 2, 4, C])
            prod_a = sb("prod_a", [128, 4, C])
            prod_b = sb("prod_b", [128, 4, C])
            halves = sb("halves", [128, CT, C])
            corr = sb("corr", [128, CT, C])
            top = sb("top", [128, CT, 16])
            neg_max, w_sum, w_inv = sb("neg_max", [128, CT]), sb("w_sum", [128, CT]), sb("w_inv", [128, CT])
            w_time = sb("w_time", [128, TT, C])
            spec_w = sb("spec_w", [128, 2, 5, C])
            spec_o = sb("spec_o", [128, 2, 4, C])
            term = sb("term", [128, 3, 2, C])
            xres = sb("xres", [128, 2, TT, C])
            v_dc = sb("v_dc", [1, 2, C])
            dc_factor = sb("dc_factor", [1, 128])

            front, back = bank[0:3], bank[3:7]

            table_loaded, dc_factor_set = sem("table_loaded"), sem("dc_factor_set")
            x_loaded = [sem("x_loaded0"), sem("x_loaded1")]
            v_loaded = [sem("v_loaded0"), sem("v_loaded1")]
            res_loaded = [sem("res_loaded0"), sem("res_loaded1")]
            x2_stored = [sem("x2_stored0"), sem("x2_stored1")]
            x_normed, q_folded, v_shifted, k_folded = sem("x_normed"), sem("q_folded"), sem("v_shifted"), sem("k_folded")
            q_made, q_used, v_made, v_copied = sem("q_made"), sem("q_used"), sem("v_made"), sem("v_copied")
            prod_made, corr_made, halves_copied = sem("prod_made"), sem("corr_made"), sem("halves_copied")
            corr_ready, top_ready, exp_made, w_made, w_scaled = (sem("corr_ready"), sem("top_ready"), sem("exp_made"),
                                                                 sem("w_made"), sem("w_scaled"))
            w_turned, w_copied, wspec_made, wspec_copied = (sem("w_turned"), sem("w_copied"), sem("wspec_made"),
                                                            sem("wspec_copied"))
            term_made, term_added, dc_added, out_made, out_used = (sem("term_made"), sem("term_added"), sem("dc_added"),
                                                                   sem("out_made"), sem("out_used"))
            x2_reduced = sem("x2_reduced")
            block = s.enter_context(nc.Block())

            LOOP = (2, STEPS - 2)

            def least(i):
                return i if isinstance(i, int) else LOOP[0]

            def most(i):
                return i if isinstance(i, int) else LOOP[1] - 1

            def steps(eng, step, after=None):
                for i in range(LOOP[0]):
                    step(i, i % 2)
                with eng.Fori(0, (LOOP[1] - LOOP[0]) // 2) as m:
                    for u in range(2):
                        step(2 * m + (LOOP[0] + u), u)
                for i in range(LOOP[1], STEPS + 1):
                    step(i, i % 2)

            OUT_ORDER = [2, 3, 0, 1]
            W_TABLES = [ER, ERZP, OR, EIZ, OI]
            V_TABLES = [ER, OR, EI, OI]
            Q_TABLES = [ER, EIZ, ERZM, OR, OI]

            @block.sync
            def _(sp):
                def load_v(i, par):
                    if least(i) >= 2:
                        sp.wait_ge(v_made, 8 * (i - 1))
                    b, c = i // NCH, (i % NCH) * C
                    sp.nop(nofuse=True)
                    sp.dma_start(vt[:, par, :, :], v_t[b, :, :, ds(c, C)]).then_inc(v_loaded[par], 16)
                    sp.dma_start(v_last[:, par, :], ctx_v[b, L - 1:L, ds(c, C)].to_broadcast([128, C]))\
                      .then_inc(v_loaded[par], 16)

                def load_x(i, par):
                    if least(i) >= 2:
                        sp.wait_ge(q_folded, 4 * (i - 1))
                    b, c = i // NCH, (i % NCH) * C
                    sp.nop(nofuse=True)
                    sp.dma_start(xt[:, par, :, :], x_t[b, :, :, ds(c, C)]).then_inc(x_loaded[par], 16)

                def load_res(i, par):
                    if least(i) >= 2:
                        sp.wait_ge(x2_stored[par], 16 * (i // 2))
                        sp.nop(nofuse=True)
                        sp.wait_ge(dc_added, 3 * (i - 1))
                    b, c = i // NCH, (i % NCH) * C
                    sp.nop(nofuse=True)
                    sp.dma_start(xres[:, par, :, :], x_t[b, :, :, ds(c, C)]).then_inc(res_loaded[par], 16)
                    sp.dma_start(v_dc[:, par, :], ctx_v[b, L - 1:L, ds(c, C)]).then_inc(res_loaded[par], 16)

                def store(i, par):
                    sp.wait_ge(x2_reduced, 4 * (i + 1))
                    b, c = i // NCH, (i % NCH) * C
                    sp.nop(nofuse=True)
                    sp.dma_start(x2_t[b, :, :, ds(c, C)], xres[:, par, :, :]).then_inc(x2_stored[par], 16)

                sp.dma_start(table[:, :], tables[:, 0:FWD + INV]).then_inc(table_loaded, 16)
                for i in range(2):
                    load_v(i, i)
                    load_x(i, i)

                def step(i, par):
                    if most(i) < STEPS:
                        load_res(i, par)
                    if most(i) + 2 < STEPS:
                        load_v(i + 2, par)
                        load_x(i + 2, par)
                    if least(i) >= 1:
                        store(i - 1, 1 - par)

                steps(sp, step)
                for par in range(2):
                    sp.wait_ge(x2_stored[par], 16 * STEPS // 2)

            @block.tensor
            def _(pe):
                def v_spectra(i, par):
                    for n in range(8):
                        if n < 4:
                            if least(i) >= 1:
                                pe.wait_ge(halves_copied, 4 * (i - 1) + n + 1)
                            if n == 0:
                                pe.wait_ge(v_shifted, 4 * i + 2)
                        else:
                            pe.wait_ge(v_copied, 8 * i + n - 3)
                            if n == 4:
                                pe.wait_ge(k_folded, 4 * (i + 1))
                        tab = V_TABLES[n % 4]
                        for j in range(2):
                            rhs = vt[:, par, 2 + j, :] if n < 4 else kf[:, j + (2 if tab >= OR else 0), :]
                            mm = pe.matmul(back[n % 4][:, :], fwd[:, tab, j, :], rhs, start=(j == 0), stop=(j == 1))
                        mm.then_inc(v_made, 1)

                def q_spectra(i):
                    for n in range(5):
                        if n >= 3:
                            pe.wait_ge(q_used, 5 * i + n - 2)
                        elif least(i) >= 2:
                            pe.wait_ge(wspec_copied, 10 * (i - 2) + n + 8)
                        elif i == 1:
                            pe.wait_ge(q_used, 5)
                        if n == 0:
                            pe.wait_ge(q_folded, 4 * i + 2)
                        if n == 3:
                            pe.wait_ge(q_folded, 4 * i + 4)
                        tab = Q_TABLES[n]
                        for j in range(2):
                            mm = pe.matmul(front[n % 3][:, :], fwd[:, tab, j, :], qf[:, j + (2 if tab >= OR else 0), :],
                                           start=(j == 0), stop=(j == 1))
                        mm.then_inc(q_made, 1)

                def turn_w(c):
                    for j in range(TT):
                        if least(c) >= 1:
                            pe.wait_ge(out_used, 4 * (c - 1) + j + 1)
                        else:
                            pe.wait_ge(v_copied, 8 + 4 + j + 1)
                        for ct in range(CT):
                            if j == 0:
                                pe.wait_ge(w_scaled, 4 * c + ct + 1)
                            mm = pe.transpose(back[j][:, ct * 128:(ct + 1) * 128], corr[:, ct, j * 128:(j + 1) * 128],
                                              ident[:, :])
                        mm.then_inc(w_turned, 1)

                def w_spectra(c):
                    for k in range(10):
                        y, tab = k // 5, W_TABLES[k % 5]
                        if k >= 3:
                            pe.wait_ge(wspec_copied, 10 * c + k - 2)
                        elif most(c) + 1 < STEPS:
                            pe.wait_ge(q_used, 5 * (c + 1) + k + 3)
                        else:
                            pe.wait_ge(wspec_copied, 10 * c)
                        if k % 5 == 0:
                            pe.wait_ge(w_copied, 4 * c + 2 * y + 2)
                        for j in range(2):
                            mm = pe.matmul(front[(5 + k) % 3][:, :], fwd[:, tab, j, :], w_time[:, 2 * y + j, :],
                                           start=(j == 0), stop=(j == 1))
                        mm.then_inc(wspec_made, 1)

                def correlate(i):
                    pe.wait_ge(prod_made, 2 * (i + 1))
                    for ct in range(CT):
                        if least(i) >= 1:
                            pe.wait_ge(w_copied, 4 * (i - 1) + ct + 1)
                        else:
                            pe.wait_ge(v_copied, 4 + ct + 1)
                        for o in range(2):
                            for k in range(2):
                                slot = o + 2 * k
                                mm = pe.matmul(back[ct][:, o * HALF:(o + 1) * HALF],
                                               prod_a[:, slot, ct * 128:(ct + 1) * 128], inv[:, slot, :],
                                               start=(k == 0), stop=(k == 1))
                        mm.then_inc(corr_made, 1)

                def out_tiles(c):
                    for j in range(TT):
                        if most(c) + 2 < STEPS:
                            pe.wait_ge(v_copied, 8 * (c + 2) + 4 + j + 1)
                        elif c + 2 == STEPS:
                            pe.wait_ge(halves_copied, 4 * (c + 1) + j + 1)
                        else:
                            pe.wait_ge(w_copied, 4 * c + j + 1)
                        if j == 0:
                            pe.wait_ge(dc_added, 3 * c + 2)
                        if j == 2:
                            pe.wait_ge(dc_added, 3 * c + 3)
                        h, p = OUT_ORDER[j] // 2, OUT_ORDER[j] % 2
                        for slot in range(4):
                            mm = pe.matmul(back[j][:, :], inv[:, slot, p * 128:(p + 1) * 128], spec_o[:, h, slot, :],
                                           start=(slot == 0), stop=(slot == 3))
                        mm.then_inc(out_made, 1)

                pe.wait_ge(table_loaded, 16)
                pe.wait_ge(ident_loaded, 16)
                v_spectra(0, 0)

                def step(i, par):
                    if most(i) < STEPS:
                        q_spectra(i)
                    if least(i) >= 1:
                        turn_w(i - 1)
                        w_spectra(i - 1)
                    if most(i) < STEPS:
                        correlate(i)
                    if most(i) + 1 < STEPS:
                        v_spectra(i + 1, 1 - par)
                    if least(i) >= 1:
                        out_tiles(i - 1)

                steps(pe, step)

            @block.scalar
            def _(act):
                def normalise(i, par):
                    act.wait_ge(x_loaded[par], 16 * (i // 2 + 1))
                    for t in range(TT):
                        row = (i // NCH) * TT + t
                        act.activation(xt[:, par, t, :], xt[:, par, t, :], ACT.Identity, bias=ln1_bias[:, ds(row, 1)],
                                       scale=ln1_scale[:, ds(row, 1)]).then_inc(x_normed, 1)

                def copy_v(i, par):
                    if least(i) >= 2:
                        act.wait_ge(term_made, 12 * (i - 1))
                    for n in range(8):
                        act.wait_ge(v_made, 8 * i + n + 1)
                        to = (spec_v1 if n < 4 else spec_v)[:, par, n % 4, :]
                        act.activation(to, back[n % 4][:, :], ACT.Copy).then_inc(v_copied, 1)

                def copy_w(c):
                    if least(c) >= 1:
                        act.wait_ge(wspec_made, 10 * c)
                    for j in range(TT):
                        act.wait_ge(w_turned, 4 * c + j + 1)
                        act.activation(w_time[:, j, :], back[j][:, :], ACT.Copy).then_inc(w_copied, 1)

                def copy_wspec(c):
                    if least(c) >= 1:
                        act.wait_ge(term_made, 12 * c)
                    for k in range(10):
                        act.wait_ge(wspec_made, 10 * c + k + 1)
                        act.activation(spec_w[:, k // 5, k % 5, :], front[(5 + k) % 3][:, :], ACT.Copy)\
                           .then_inc(wspec_copied, 1)

                def copy_halves(i):
                    if least(i) >= 1:
                        act.wait_ge(w_made, 4 * i)
                    for ct in range(CT):
                        act.wait_ge(corr_made, 4 * i + ct + 1)
                        act.activation(halves[:, ct, :], back[ct][:, :], ACT.Copy).then_inc(halves_copied, 1)

                def weigh(i):
                    act.wait_ge(top_ready, 1 + 4 * i)
                    for ct in range(CT):
                        act.activation(halves[:, ct, :], corr[:, ct, :], ACT.Exp, bias=neg_max[:, ct:ct + 1])\
                           .then_inc(exp_made, 1)
                    act.wait_ge(top_ready, 4 * (i + 1))
                    for ct in range(CT):
                        act.activation(corr[:, ct, :], corr[:, ct, :], ACT.Copy, scale=w_inv[:, ct:ct + 1])\
                           .then_inc(w_scaled, 1)

                normalise(0, 0)
                copy_v(0, 0)

                def step(i, par):
                    if least(i) >= 1:
                        copy_w(i - 1)
                        copy_wspec(i - 1)
                    if most(i) < STEPS:
                        copy_halves(i)
                    if most(i) + 1 < STEPS:
                        normalise(i + 1, 1 - par)
                        copy_v(i + 1, 1 - par)
                    if most(i) < STEPS:
                        weigh(i)

                steps(act, step)

            @block.vector
            def _(dve):
                def q_times_k(i, par):
                    dve.wait_ge(v_copied, 8 * (i + 1))
                    if least(i) >= 1:
                        dve.wait_ge(corr_made, 4 * i)
                    k = spec_v[:, par]
                    uses = [[(prod_a, 0, 0)], [(prod_b, 0, 2), (prod_a, 2, 0)], [(prod_b, 2, 2)],
                            [(prod_a, 1, 1), (prod_b, 3, 3)], [(prod_b, 1, 3), (prod_a, 3, 1)]]
                    for n in range(5):
                        dve.wait_ge(q_made, 5 * i + n + 1)
                        for to, slot, kslot in uses[n]:
                            op = dve.tensor_tensor(to[:, slot, :], front[n % 3][:, :], k[:, kslot, :], ALU.mult)
                        op.then_inc(q_used, 1)

                def v_times_w(c, par):
                    v1r, v1i = spec_v1[:, par, 0:2, :], spec_v1[:, par, 2:4, :]
                    vr, vi = spec_v[:, par, 0:2, :], spec_v[:, par, 2:4, :]
                    r, rz, im = ([spec_w[:, y, 0:3:2, :] for y in range(2)], [spec_w[:, y, 1:3, :] for y in range(2)],
                                 [spec_w[:, y, 3:5, :] for y in range(2)])
                    o1r, o1i, o0r, o0i = spec_o[:, 1, 0:2, :], spec_o[:, 1, 2:4, :], spec_o[:, 0, 0:2, :], spec_o[:, 0, 2:4, :]
                    todo = [(o1r, v1r, r[0]), (None, v1i, im[0]), (o1i, v1i, rz[0]), (None, v1r, im[0]),
                            (o0r, vr, r[0]), (None, vi, im[0]), (o0i, vi, rz[0]), (None, vr, im[0]),
                            (None, v1r, r[1]), (None, v1i, rz[1]), (None, v1i, im[1]), (None, v1r, im[1])]
                    if least(c) >= 1:
                        dve.wait_ge(out_made, 4 * c)
                        dve.wait_ge(term_added, 8 * c)
                    dve.wait_ge(wspec_copied, 10 * c + 5)
                    t = 0
                    for n, (to, a, w) in enumerate(todo):
                        if n == 8:
                            dve.wait_ge(wspec_copied, 10 * c + 10)
                        if to is None:
                            if t >= 3:
                                dve.wait_ge(term_added, 8 * c + t - 2)
                            to = term[:, t % 3]
                            t += 1
                        dve.tensor_tensor(to, a, w, ALU.mult).then_inc(term_made, 1)

                def top_k(i):
                    if least(i) >= 1:
                        dve.wait_ge(w_turned, 4 * i)
                    dve.wait_ge(prod_made, 2 * (i + 1))
                    for ct in range(CT):
                        e, o = halves[:, ct, 0:HALF], halves[:, ct, HALF:C]
                        dve.wait_ge(halves_copied, 4 * i + ct + 1)
                        dve.tensor_tensor(corr[:, ct, 0:HALF], e, o, ALU.add).then_inc(corr_ready, 1)
                        dve.tensor_tensor(corr[:, ct, HALF:C], e, o, ALU.subtract).then_inc(corr_ready, 1)
                    base = 20 * i
                    for ct in range(CT):
                        dve.wait_ge(corr_ready, base + 2 * ct + 2)
                        dve.nop(nofuse=True)
                        dve.max(top[:, ct, 0:8], corr[:, ct, :]).then_inc(corr_ready, 1)
                    dve.wait_ge(corr_ready, base + 12)
                    dve.tensor_scalar(neg_max[:, :], top[:, :, 0], -1.0, None, ALU.mult).then_inc(top_ready, 1)
                    for ct in range(CT):
                        dve.match_replace(prod_b[:, ct, :], top[:, ct, 0:8], corr[:, ct, :], -3.0e38)\
                           .then_inc(corr_ready, 1)
                    for ct in range(CT):
                        dve.wait_ge(corr_ready, base + 12 + ct + 1)
                        dve.nop(nofuse=True)
                        dve.max(top[:, ct, 8:16], prod_b[:, ct, :]).then_inc(corr_ready, 1)
                    for ct in range(CT):
                        dve.wait_ge(corr_ready, base + 16 + ct + 1)
                        dve.wait_ge(exp_made, 4 * i + ct + 1)
                        dve.scalar_tensor_tensor(out=corr[:, ct, :], in0=corr[:, ct, :], scalar=top[:, ct, TOPK - 1:TOPK],
                                                 in1=halves[:, ct, :], op0=ALU.is_ge, op1=ALU.mult,
                                                 accum_out=w_sum[:, ct:ct + 1]).then_inc(w_made, 1)
                    dve.wait_ge(w_made, 4 * (i + 1))
                    dve.reciprocal(w_inv[:, :], w_sum[:, :]).then_inc(top_ready, 3)

                def residual(c, par):
                    dve.wait_ge(res_loaded[par], 32 * (c // 2 + 1))
                    row, chunk = (c // NCH) * TT, c % NCH
                    for j in range(TT):
                        t = OUT_ORDER[j]
                        dve.wait_ge(out_made, 4 * c + j + 1)
                        dve.scalar_tensor_tensor(out=xres[:, par, t, :], in0=back[j][:, :], scalar=gates[:, 0:1],
                                                 in1=xres[:, par, t, :], op0=ALU.mult, op1=ALU.add).then_inc(out_used, 1)
                    for j in range(TT):
                        t = OUT_ORDER[j]
                        dve.wait_ge(out_used, 4 * c + j + 1)
                        dve.bn_stats(x2_stats[:, row + t, chunk, :], xres[:, par, t, :]).then_inc(x2_reduced, 1)

                def step(i, par):
                    if most(i) < STEPS:
                        q_times_k(i, par)
                    if least(i) >= 1:
                        v_times_w(i - 1, 1 - par)
                    if most(i) < STEPS:
                        top_k(i)
                    if least(i) >= 1:
                        residual(i - 1, 1 - par)

                dve.wait_ge(gates_ready, 1)
                steps(dve, step)

            @block.gpsimd
            def _(pool):
                def prepare_v(i, par):
                    pool.wait_ge(v_loaded[par], 32 * (i // 2 + 1))
                    if least(i) >= 1:
                        pool.wait_ge(v_made, 8 * i)
                    for t in (2, 3, 0, 1):
                        pool.tensor_tensor(vt[:, par, t, :], vt[:, par, t, :], v_last[:, par, :], ALU.subtract)\
                            .then_inc(v_shifted, 1)
                    pool.wait_ge(v_shifted, 4 * (i + 1))
                    for j in range(4):
                        pool.tensor_tensor(kf[:, j, :], vt[:, par, j % 2, :], vt[:, par, 2 + j % 2, :],
                                           ALU.add if j < 2 else ALU.subtract).then_inc(k_folded, 1)

                def fold_q(i, par):
                    if least(i) >= 1:
                        pool.wait_ge(q_made, 5 * i)
                    pool.wait_ge(x_normed, 4 * (i + 1))
                    for j in range(4):
                        pool.tensor_tensor(qf[:, j, :], xt[:, par, j % 2, :], xt[:, par, 2 + j % 2, :],
                                           ALU.add if j < 2 else ALU.subtract).then_inc(q_folded, 1)

                def sum_qk(i):
                    pool.wait_ge(q_used, 5 * (i + 1))
                    pool.tensor_tensor(prod_a[:, 0:2, :], prod_a[:, 0:2, :], prod_b[:, 0:2, :], ALU.add)\
                        .then_inc(prod_made, 1)
                    pool.tensor_tensor(prod_a[:, 2:4, :], prod_a[:, 2:4, :], prod_b[:, 2:4, :], ALU.subtract)\
                        .then_inc(prod_made, 1)

                def sum_vw(c, par):
                    o1r, o1i, o0r, o0i = spec_o[:, 1, 0:2, :], spec_o[:, 1, 2:4, :], spec_o[:, 0, 0:2, :], spec_o[:, 0, 2:4, :]
                    todo = [(o1r, ALU.add, 2, 0), (o1i, ALU.subtract, 4, 0), (o0r, ALU.add, 6, 0),
                            (o0i, ALU.subtract, 8, 0), (o0r, ALU.add, 9, 3), (o0i, ALU.add, 10, 4),
                            (o0r, ALU.add, 11, 5), (o0i, ALU.subtract, 12, 6)]
                    pool.wait_ge(res_loaded[par], 32 * (c // 2 + 1))
                    dc_row = v_dc[:, par, :].rearrange("p (a c) -> p a c", c=128)
                    pool.tensor_tensor(dc_row, dc_row, dc_factor[:, :].rearrange("p (a c) -> p a c", a=1).to_broadcast([1, CT, 128]),
                                       ALU.mult).then_inc(dc_added, 1)
                    for t, (to, sign, made, own) in enumerate(todo):
                        pool.wait_ge(term_made, 12 * c + made)
                        if own:
                            pool.wait_ge(term_added, 8 * c + own)
                        pool.tensor_tensor(to, to, term[:, t % 3], sign).then_inc(term_added, 1)
                        if t in (1, 7):
                            if t == 1:
                                pool.wait_ge(dc_added, 3 * c + 1)
                            pool.wait_ge(term_added, 8 * c + t + 1)
                            dc = spec_o[0:1, 1 if t == 1 else 0, 0, :]
                            pool.tensor_tensor(dc, dc, v_dc[:, par, :], ALU.add).then_inc(dc_added, 1)

                pool.memset(dc_factor[:, :], float(L)).then_inc(dc_factor_set, 1)
                pool.wait_ge(dc_factor_set, 1)
                prepare_v(0, 0)
                fold_q(0, 0)

                def step(i, par):
                    if most(i) < STEPS:
                        sum_qk(i)
                    if most(i) + 1 < STEPS:
                        prepare_v(i + 1, 1 - par)
                    if least(i) >= 1:
                        sum_vw(i - 1, 1 - par)
                    if most(i) + 1 < STEPS:
                        fold_q(i + 1, 1 - par)

                steps(pool, step)

        with ExitStack() as s:
            def sb(name, shape, dt=f32):
                return s.enter_context(nc.sbuf_tensor(name, shape, dt))

            w_hi, w_lo = sb("w_hi", [128, KD, D], f16), sb("w_lo", [128, KD, D], f16)
            ag_hi, ag_lo = sb("ag_hi", [128, KD, NG], f16), sb("ag_lo", [128, KD, NG], f16)
            b_hi, b_lo = sb("b_hi", [128, D], f16), sb("b_lo", [128, D], f16)
            row = sb("row", [128, 2, D])
            norm = sb("norm", [128, D])
            nt_hi, nt_lo = sb("nt_hi", [128, 2, KD, 128], f16), sb("nt_lo", [128, 2, KD, 128], f16)
            bias = sb("bias", [128, D])
            ln2_scale, ln2_bias = sb("ln2_scale", [128, ROWS]), sb("ln2_bias", [128, ROWS])
            mv = sb("mv2", [128, ROWS, 2])
            var, std, tmp = sb("var2", [128, ROWS]), sb("std2", [128, ROWS]), sb("tmp2", [128, ROWS])
            thr_b, out_gate = sb("thr_b", [128, 1]), sb("out_gate", [128, 1])
            logit = sb("logit", [128, NG])
            lmax, esum, erec, wsum, wzero = (sb(n, [128, 1]) for n in ("lmax", "esum", "erec", "wsum", "wzero"))
            thr = sb("thr", [128, 1])
            gate = sb("gate", [128, E])
            hw = sb("hw", [128, E * R])
            hwt_hi, hwt_lo = sb("hwt_hi", [128, 128], f16), sb("hwt_lo", [128, 128], f16)

            row_loaded = [sem("wrow_loaded0"), sem("wrow_loaded1")]
            small_loaded, b_loaded = sem("small_loaded"), sem("b_loaded")
            wt_made, wt_hi, wt_lo = sem("wt_made"), sem("wt_hi"), sem("wt_lo")
            ln2_step, ln2_sqrt, bias_ready = sem("ln2_step"), sem("ln2_sqrt"), sem("bias_ready")

            NW = D // 128
            JOBS = NW + 2
            DESCALE = 1.0 / (N_SCALE * W_SCALE)

            def weight_target(n, q, part):
                if n < NW:
                    return (w_hi, w_lo)[part][:, 4 * q:4 * q + 4, n * 128:(n + 1) * 128]
                t = (ag_hi, ag_lo)[part]
                return t[:, 4 * q:4 * q + 4, 0:128] if n == NW else t[:, 4 * q:4 * q + 4, 128:NG]

            def weight_bank(n, q):
                cols = 128 if n <= NW else E + 1
                view = bank[(4 * n + q) % 8][:, 0:4 * cols] if cols == 128 else bank[(4 * n + q) % 8][:, 0:4 * 16]
                view = view.rearrange("p (k c) -> p k c", k=4)
                return view if cols == 128 else view[:, :, 0:cols]

            with nc.Block() as block:
                @block.sync
                def _(sp):
                    sp.dma_start(bias[:, :], b_base.rearrange("(a n) -> a n", a=1).to_broadcast([128, D])).then_inc(small_loaded, 16)
                    sp.dma_start(thr_b[:, :], b_thr.to_broadcast([128, 1])).then_inc(small_loaded, 16)
                    b_view = norm[:, :].rearrange("p (n e r) -> p n e r", e=E, r=R)
                    for e in range(E):
                        sp.dma_start(b_view[:, :, e, :], b_w[e].rearrange("(n p) r -> p n r", p=128)).then_inc(b_loaded, 16)
                    for n in range(JOBS):
                        if n >= 2:
                            sp.wait_ge(wt_made, 4 * (n - 1))
                        if n < NW:
                            sp.dma_start(row[:, n % 2, :], w_base[n * 128:(n + 1) * 128, :]).then_inc(row_loaded[n % 2], 16)
                        elif n == NW:
                            sp.dma_start(row[:, n % 2, :], a_w.rearrange("e r d -> (e r) d")).then_inc(row_loaded[n % 2], 16)
                        else:
                            sp.dma_start(row[0:E, n % 2, :], w_gate).then_inc(row_loaded[n % 2], 16)
                            sp.dma_start(row[E:E + 1, n % 2, :], w_thr.rearrange("(a n) -> a n", a=1)).then_inc(row_loaded[n % 2], 16)

                @block.tensor
                def _(pe):
                    for n in range(JOBS):
                        pe.wait_ge(row_loaded[n % 2], 16 * (n // 2 + 1) + (16 if n == JOBS - 1 else 0))
                        rows = 128 if n <= NW else E + 1
                        for q in range(4):
                            if 4 * n + q >= 8:
                                pe.wait_ge(wt_hi, 4 * n + q - 7)
                                pe.wait_ge(wt_lo, 4 * n + q - 7)
                            view = weight_bank(n, q)
                            for k in range(4):
                                d = (4 * q + k) * 128
                                mm = pe.transpose(view[:, k, :], row[0:rows, n % 2, d:d + 128], ident[0:rows, 0:rows])
                            mm.then_inc(wt_made, 1)
                    pe.wait_ge(b_loaded, 16 * E)
                    for q in range(4):
                        g = 4 * JOBS + q
                        pe.wait_ge(wt_hi, g - 7)
                        pe.wait_ge(wt_lo, g - 7)
                        for k in range(4):
                            mm = pe.transpose(bank[g % 8][:, k * 128:(k + 1) * 128], norm[:, (4 * q + k) * 128:(4 * q + k + 1) * 128],
                                              ident[:, :])
                        mm.then_inc(wt_made, 1)

                @block.scalar
                def _(act):
                    for g in range(4 * JOBS + 4):
                        act.wait_ge(wt_made, g + 1)
                        if g < 4 * JOBS:
                            to, view = weight_target(g // 4, g % 4, 0), weight_bank(g // 4, g % 4)
                        else:
                            q = g - 4 * JOBS
                            to, view = b_hi[:, q * 512:(q + 1) * 512], bank[g % 8][:, :]
                        act.activation(to, view, ACT.Copy, scale=W_SCALE).then_inc(wt_hi, 1)
                    act.wait_ge(ln2_step, 1)
                    act.activation(std[:, :], var[:, :], ACT.Sqrt).then_inc(ln2_sqrt, 1)

                @block.vector
                def _(dve):
                    for g in range(4 * JOBS + 4):
                        dve.wait_ge(wt_hi, g + 1)
                        if g < 4 * JOBS:
                            hi, lo, view = (weight_target(g // 4, g % 4, 0), weight_target(g // 4, g % 4, 1),
                                            weight_bank(g // 4, g % 4))
                        else:
                            q = g - 4 * JOBS
                            hi, lo, view = b_hi[:, q * 512:(q + 1) * 512], b_lo[:, q * 512:(q + 1) * 512], bank[g % 8][:, :]
                        dve.scalar_tensor_tensor(out=lo, in0=view, scalar=W_SCALE, in1=hi, op0=ALU.mult, op1=ALU.subtract)\
                           .then_inc(wt_lo, 1)
                    for r in range(ROWS):
                        op = dve.bn_aggr(mv[:, r, :], x2_stats[:, r, :, :].rearrange("p a b -> p (a b)"))
                    op.then_inc(wt_lo, 1)
                    dve.wait_ge(wt_lo, 4 * JOBS + 5)
                    dve.tensor_scalar(var[:, :], mv[:, :, 1], EPS, None, ALU.add).then_inc(ln2_step, 1)
                    newton(dve, ln2_step, 1, ln2_sqrt, 1, var, std, tmp, mv[:, :, 0], ln2_scale, ln2_bias, N_SCALE)
                    dve.wait_ge(small_loaded, 32)
                    dve.tensor_scalar(bias[:, :], bias[:, :], gates[:, 1:2], None, ALU.mult).then_inc(bias_ready, 1)
                    dve.tensor_scalar(out_gate[:, :], gates[:, 1:2], DESCALE, None, ALU.mult).then_inc(bias_ready, 1)
                    dve.tensor_scalar(thr_b[:, :], thr_b[:, :], -1.0, None, ALU.mult).then_inc(bias_ready, 1)

            x2_loaded = [sem("x2_loaded0"), sem("x2_loaded1")]
            out_stored = [sem("out_stored0"), sem("out_stored1")]
            normed, turned, nt_hi_made, nt_lo_made = sem("normed"), sem("turned"), sem("nt_hi_made"), sem("nt_lo_made")
            logits_made, logits_copied, exps_made, gate_step = (sem("logits_made"), sem("logits_copied"),
                                                                sem("exps_made"), sem("gate_step"))
            hw_turned, hwt_hi_made, hwt_lo_made = sem("hw_turned"), sem("hwt_hi_made"), sem("hwt_lo_made")
            bias_added, dense_made, out_ready = sem("bias_added"), sem("dense_made"), sem("out_ready")
            dense, turn_bank, logit_bank, hw_bank = bank[0:4], bank[4:6], bank[6], bank[7]
            GATE_OPS = 11

            FLOOP = (2, ROWS - 2)

            def fleast(i):
                return i if isinstance(i, int) else FLOOP[0]

            def fmost(i):
                return i if isinstance(i, int) else FLOOP[1] - 1

            def tiles(eng, step):
                for i in range(FLOOP[0]):
                    step(i, i % 2)
                with eng.Fori(0, (FLOOP[1] - FLOOP[0]) // 2) as m:
                    for u in range(2):
                        step(2 * m + (FLOOP[0] + u), u)
                for i in range(FLOOP[1], ROWS):
                    step(i, i % 2)

            with nc.Block() as block:
                @block.sync
                def _(sp):
                    def load(i, par):
                        if fleast(i) >= 2:
                            sp.wait_ge(out_stored[par], 16 * (i // 2))
                        sp.nop(nofuse=True)
                        sp.dma_start(row[:, par, :], x2_rows[i]).then_inc(x2_loaded[par], 16)

                    def step(i, par):
                        if fmost(i) + 1 < ROWS:
                            load(i + 1, 1 - par)
                        sp.wait_ge(out_ready, 4 * (i + 1))
                        sp.nop(nofuse=True)
                        sp.dma_start(out_rows[i], row[:, par, :]).then_inc(out_stored[par], 16)

                    load(0, 0)
                    tiles(sp, step)
                    for par in range(2):
                        sp.wait_ge(out_stored[par], 16 * ROWS // 2)

                @block.tensor
                def _(pe):
                    def turn(i):
                        pe.wait_ge(normed, i + 1)
                        for q in range(4):
                            if q >= 2 or fleast(i) >= 1:
                                pe.wait_ge(nt_hi_made, 4 * i + q - 1)
                                pe.wait_ge(nt_lo_made, 4 * i + q - 1)
                            for k in range(4):
                                d = (4 * q + k) * 128
                                mm = pe.transpose(turn_bank[q % 2][:, k * 128:(k + 1) * 128], norm[:, d:d + 128], ident[:, :])
                            mm.then_inc(turned, 1)

                    def logits(i, par):
                        if fleast(i) >= 1:
                            pe.wait_ge(logits_copied, i)
                        pe.wait_ge(nt_hi_made, 4 * (i + 1))
                        pe.wait_ge(nt_lo_made, 4 * (i + 1))
                        acc = logit_bank[:, 0:NG]
                        for k in range(KD):
                            pe.matmul(acc, nt_hi[:, par, k, :], ag_hi[:, k, :], start=(k == 0), stop=False)
                            pe.matmul(acc, nt_hi[:, par, k, :], ag_lo[:, k, :], start=False, stop=False)
                            mm = pe.matmul(acc, nt_lo[:, par, k, :], ag_hi[:, k, :], start=False, stop=(k == KD - 1))
                        mm.then_inc(logits_made, 1)

                    def base(i, par):
                        for k in range(KD):
                            for n, (a, w) in enumerate(((nt_hi, w_hi), (nt_hi, w_lo), (nt_lo, w_hi))):
                                for o in range(4):
                                    if k == 0 and n == 0 and fleast(i) >= 1:
                                        pe.wait_ge(out_ready, 4 * (i - 1) + o + 1)
                                    pe.matmul(dense[o][:, :], a[:, par, k, :], w[:, k, o * 512:(o + 1) * 512],
                                              start=(k == 0 and n == 0), stop=False)

                    def experts(i):
                        pe.wait_ge(gate_step, GATE_OPS * (i + 1))
                        if fleast(i) >= 1:
                            pe.wait_ge(hwt_lo_made, i)
                        pe.transpose(hw_bank[:, 0:128], hw[:, :], ident[:, :]).then_inc(hw_turned, 1)
                        pe.wait_ge(hwt_hi_made, i + 1)
                        pe.wait_ge(hwt_lo_made, i + 1)
                        for o in range(4):
                            cols = slice(o * 512, (o + 1) * 512)
                            pe.matmul(dense[o][:, :], hwt_hi[:, :], b_hi[:, cols], start=False, stop=False)
                            pe.matmul(dense[o][:, :], hwt_hi[:, :], b_lo[:, cols], start=False, stop=False)
                            pe.matmul(dense[o][:, :], hwt_lo[:, :], b_hi[:, cols], start=False, stop=True)\
                              .then_inc(dense_made, 1)

                    def step(i, par):
                        logits(i, par)
                        if fmost(i) + 1 < ROWS:
                            turn(i + 1)
                        base(i, par)
                        experts(i)

                    turn(0)
                    tiles(pe, step)

                @block.scalar
                def _(act):
                    def normalise(i, par):
                        act.wait_ge(x2_loaded[par], 16 * (i // 2 + 1))
                        if fleast(i) >= 1:
                            act.wait_ge(turned, 4 * i)
                        act.activation(norm[:, :], row[:, par, :], ACT.Identity, bias=ln2_bias[:, ds(i, 1)],
                                       scale=ln2_scale[:, ds(i, 1)]).then_inc(normed, 1)

                    def turned_hi(i, par):
                        if fleast(i) >= 2:
                            act.wait_ge(dense_made, 4 * (i - 1))
                        for q in range(4):
                            act.wait_ge(turned, 4 * i + q + 1)
                            act.activation(nt_hi[:, par, 4 * q:4 * q + 4, :].rearrange("p k t -> p (k t)"),
                                           turn_bank[q % 2][:, :], ACT.Copy).then_inc(nt_hi_made, 1)

                    def gating(i):
                        act.wait_ge(logits_made, i + 1)
                        if fleast(i) >= 1:
                            act.wait_ge(gate_step, GATE_OPS * i)
                        act.activation(logit[:, :], logit_bank[:, 0:NG], ACT.Copy, scale=DESCALE)\
                           .then_inc(logits_copied, 1)
                        act.wait_ge(gate_step, GATE_OPS * i + 1)
                        act.wait_ge(logits_copied, i + 1)
                        act.activation(gate[:, :], logit[:, E * R:E * R + E], ACT.Exp, bias=lmax[:, :],
                                       accum_out=esum[:, :]).then_inc(exps_made, 1)
                        act.activation(thr[:, :], logit[:, E * R + E:NG], ACT.Exp, bias=thr_b[:, :], scale=-1.0)\
                           .then_inc(exps_made, 1)

                    def hw_hi(i):
                        if fleast(i) >= 1:
                            act.wait_ge(dense_made, 4 * i)
                        act.wait_ge(hw_turned, i + 1)
                        act.activation(hwt_hi[:, :], hw_bank[:, 0:128], ACT.Copy).then_inc(hwt_hi_made, 1)

                    def step(i, par):
                        gating(i)
                        if fmost(i) + 1 < ROWS:
                            normalise(i + 1, 1 - par)
                            turned_hi(i + 1, 1 - par)
                        hw_hi(i)

                    normalise(0, 0)
                    turned_hi(0, 0)
                    tiles(act, step)

                @block.vector
                def _(dve):
                    def turned_lo(i, par):
                        if fleast(i) >= 2:
                            dve.wait_ge(dense_made, 4 * (i - 1))
                        for q in range(4):
                            dve.wait_ge(nt_hi_made, 4 * i + q + 1)
                            dve.tensor_tensor(nt_lo[:, par, 4 * q:4 * q + 4, :].rearrange("p k t -> p (k t)"),
                                              turn_bank[q % 2][:, :],
                                              nt_hi[:, par, 4 * q:4 * q + 4, :].rearrange("p k t -> p (k t)"),
                                              ALU.subtract).then_inc(nt_lo_made, 1)

                    def gating(i):
                        done = [0]

                        def chain(op):
                            op.then_inc(gate_step, 1)
                            done[0] += 1
                            if done[0] < GATE_OPS:
                                dve.wait_ge(gate_step, GATE_OPS * i + done[0])

                        dve.wait_ge(logits_copied, i + 1)
                        chain(dve.tensor_reduce(lmax[:, :], logit[:, E * R:E * R + E], AX.X, ALU.max, negate=True))
                        dve.wait_ge(exps_made, 2 * (i + 1))
                        chain(dve.reciprocal(erec[:, :], esum[:, :]))
                        chain(dve.tensor_scalar(thr[:, :], thr[:, :], 1.0, 1.0 / MAX_THRESHOLD, ALU.add, ALU.mult))
                        chain(dve.reciprocal(thr[:, :], thr[:, :]))
                        chain(dve.tensor_scalar(gate[:, :], gate[:, :], erec[:, :], thr[:, :], ALU.mult, ALU.subtract))
                        chain(dve.tensor_scalar(gate[:, :], gate[:, :], 0.0, None, ALU.max, ALU.add, accum_out=wsum[:, :]))
                        chain(dve.tensor_scalar(wzero[:, :], wsum[:, :], 0.0, None, ALU.is_equal))
                        chain(dve.tensor_tensor(wsum[:, :], wsum[:, :], wzero[:, :], ALU.add))
                        chain(dve.reciprocal(wsum[:, :], wsum[:, :]))
                        chain(dve.tensor_scalar(gate[:, :], gate[:, :], wsum[:, :], SCALING * N_SCALE, ALU.mult, ALU.mult))
                        if fleast(i) >= 1:
                            dve.wait_ge(hw_turned, i)
                        chain(dve.tensor_tensor(hw[:, :].rearrange("p (e r) -> p e r", e=E),
                                                logit[:, 0:E * R].rearrange("p (e r) -> p e r", e=E),
                                                gate[:, :].rearrange("p (e r) -> p e r", r=1).to_broadcast([128, E, R]),
                                                ALU.mult))

                    def hw_lo(i):
                        if fleast(i) >= 1:
                            dve.wait_ge(dense_made, 4 * i)
                        dve.wait_ge(hwt_hi_made, i + 1)
                        dve.tensor_tensor(hwt_lo[:, :], hw_bank[:, 0:128], hwt_hi[:, :], ALU.subtract).then_inc(hwt_lo_made, 1)

                    def finish(i, par):
                        dve.wait_ge(bias_added, i + 1)
                        for o in range(4):
                            cols = slice(o * 512, (o + 1) * 512)
                            dve.wait_ge(dense_made, 4 * i + o + 1)
                            dve.scalar_tensor_tensor(out=row[:, par, cols], in0=dense[o][:, :], scalar=out_gate[:, :],
                                                     in1=row[:, par, cols], op0=ALU.mult, op1=ALU.add).then_inc(out_ready, 1)

                    def step(i, par):
                        gating(i)
                        if fmost(i) + 1 < ROWS:
                            turned_lo(i + 1, 1 - par)
                        hw_lo(i)
                        finish(i, par)

                    turned_lo(0, 0)
                    tiles(dve, step)

                @block.gpsimd
                def _(pool):
                    def step(i, par):
                        pool.wait_ge(normed, i + 1)
                        pool.tensor_tensor(row[:, par, :], row[:, par, :], bias[:, :], ALU.add).then_inc(bias_added, 1)

                    pool.wait_ge(bias_ready, 3)
                    tiles(pool, step)


_INS = ['x', 'ctx_4096', 'g_xattn', 'g_ffn', 'L0_ffn_W_base', 'L0_ffn_b_base', 'L0_ffn_W_gate', 'L0_ffn_W_thr',
        'L0_ffn_b_thr', 'L0_ffn_A_w', 'L0_ffn_B_w']


def kernel(**inputs):
    import concourse.bacc as _bacc
    from concourse.bass_utils import run_bass_kernel_spmd as _run

    nc = _bacc.Bacc("TRN2", target_bir_lowering=False, num_devices=1)
    arrays, args = {}, []
    for name, a in [(n, inputs[n]) for n in _INS] + [("tables", dft_tables())]:
        a = np.ascontiguousarray(a)
        arrays[f"in_{name}_dram"] = a
        args.append(nc.dram_tensor(f"in_{name}_dram", a.shape, mybir.dt.from_np(a.dtype), kind="ExternalInput").ap())
    out = nc.dram_tensor("out_0_dram", (B, L, D), mybir.dt.float32, kind="ExternalOutput").ap()
    flamingo_kernel(nc, *args, out)
    r = _run(nc, [arrays], core_ids=[0])
    return r.results[0]["out_0_dram"]
```

```python
import concourse.bass as bass
from concourse import mybir
from contextlib import ExitStack
import numpy as np

B, L, D = 8, 512, 2048
C = 512
HALF = L // 2
TT = L // 128
NCH = D // C
STEPS = B * NCH
CT = C // 128
TOPK = int(2 * np.log(L))
EPS = 1e-5
ROWS = B * L // 128
E, R = 8, 16
KD = D // 128
NG = E * R + E + 1
SCALING = 2.0
MAX_THRESHOLD = 0.125
N_SCALE, W_SCALE = 16.0, 64.0

ER, EI, EIZ, ERZM, ERZP, OR, OI = range(7)
FWD = 7 * 2 * 128
INV = 4 * HALF
T_SCALE = 16.0
P_SCALE = 1.0 / L
V_SCALE = P_SCALE / T_SCALE


def split16(a):
    hi = a.astype(np.float16)
    return np.stack([hi, (a - hi).astype(np.float16)], axis=1)


def dft_tables():
    t = np.arange(HALF)[:, None].astype(np.float64)
    g = np.arange(128)[None, :].astype(np.float64)
    even, odd = 2 * np.pi * g * t / HALF, 2 * np.pi * (2 * g + 1) * t / L
    nyquist = np.cos(np.pi * t[:, 0])
    er, eiz, o_r, oi = np.cos(even), -np.sin(even), np.cos(odd), -np.sin(odd)
    ei, erzm, erzp = eiz.copy(), er.copy(), er.copy()
    ei[:, 0], erzm[:, 0], erzp[:, 0] = nyquist, -nyquist, nyquist
    fwd = np.stack([er, ei, eiz, erzm, erzp, o_r, oi])
    fwd = fwd.reshape(7, 2, 128, 128).transpose(2, 0, 1, 3).reshape(128, FWD)
    ier, iei, ior, ioi = 2 * er.T / L, 2 * eiz.T / L, 2 * o_r.T / L, 2 * oi.T / L
    ier[0] /= 2
    iei[0] = nyquist / L
    inv = np.stack([ier, ior, iei, ioi], axis=1).reshape(128, INV)
    exact = np.concatenate([inv, np.eye(128)], axis=1).astype(np.float32)
    halves = np.concatenate([split16(fwd * T_SCALE).reshape(128, -1), split16(inv * (L * T_SCALE)).reshape(128, -1)], axis=1)
    return exact, halves




def newton(dve, step, done, sqrt_done, sqrt_n, var, std, tmp, mean, scale, bias, factor):
    ALU = mybir.AluOpType
    dve.wait_ge(sqrt_done, sqrt_n)
    dve.reciprocal(scale[:, :], std[:, :]).then_inc(step, 1)
    dve.wait_ge(step, done + 1)
    dve.tensor_tensor(tmp[:, :], scale[:, :], scale[:, :], ALU.mult).then_inc(step, 1)
    dve.wait_ge(step, done + 2)
    dve.tensor_tensor(tmp[:, :], tmp[:, :], var[:, :], ALU.mult).then_inc(step, 1)
    dve.wait_ge(step, done + 3)
    dve.tensor_scalar(tmp[:, :], tmp[:, :], -0.5 * factor, 1.5 * factor, ALU.mult, ALU.add).then_inc(step, 1)
    dve.wait_ge(step, done + 4)
    dve.tensor_tensor(scale[:, :], scale[:, :], tmp[:, :], ALU.mult).then_inc(step, 1)
    dve.wait_ge(step, done + 5)
    dve.scalar_tensor_tensor(out=bias[:, :], in0=mean, scalar=-1.0, in1=scale[:, :],
                             op0=ALU.mult, op1=ALU.mult).then_inc(step, 1)


def flamingo_kernel(nc, x, ctx_v, g_xattn, g_ffn, w_base, b_base, w_gate, w_thr, b_thr, a_w, b_w,
                    tables, tables16, out):
    f32, f16 = mybir.dt.float32, mybir.dt.float16
    ALU, ACT, AX = mybir.AluOpType, mybir.ActivationFunctionType, mybir.AxisListType
    ds = bass.ds

    x2 = nc.dram_tensor("x2_scratch", (B, L, D), f32, kind="Internal").ap()
    x_t = x.rearrange("b (k p) c -> b p k c", p=128)
    v_t = ctx_v.rearrange("b (k p) c -> b p k c", p=128)
    x2_t = x2.rearrange("b (k p) c -> b p k c", p=128)
    x_rows = x.rearrange("b (k p) c -> (b k) p c", p=128)
    x2_rows = x2.rearrange("b (k p) c -> (b k) p c", p=128)
    out_rows = out.rearrange("b (k p) c -> (b k) p c", p=128)

    whole = ExitStack()
    with whole:
        def sem(name):
            return whole.enter_context(nc.semaphore(name))

        def keep(name, shape, dt=f32):
            return whole.enter_context(nc.sbuf_tensor(name, shape, dt))

        ident = keep("ident", [128, 128])
        gates_raw = keep("gates_raw", [128, 2])
        gates = keep("gates", [128, 2])
        norm = keep("norm", [128, D])
        bank = [whole.enter_context(nc.psum_tensor(f"bank{n}", [128, 512], f32)) for n in range(8)]

        b_loaded = sem("b_loaded")
        ident_loaded, gates_loaded, gates_ready = sem("ident_loaded"), sem("gates_loaded"), sem("gates_ready")

        with ExitStack() as s:
            def sb(name, shape, dt=f32):
                return s.enter_context(nc.sbuf_tensor(name, shape, dt))

            def both(t):
                return t[:, :].bitcast(f16).rearrange("p (h a c) -> p h a c", h=2, a=4)

            def four(t):
                return t[:, :].rearrange("p (a c) -> p a c", a=4)

            table = sb("table", [128, INV])
            table16 = sb("table16", [128, 2 * (FWD + INV)], f16)
            inv = table[:, :].rearrange("p (a q) -> p a q", a=4)
            fwd16 = table16[:, 0:2 * FWD].rearrange("p (h a j g) -> p h a j g", h=2, a=7, j=2)
            inv16 = table16[:, 2 * FWD:2 * (FWD + INV)].rearrange("p (h a q) -> p h a q", h=2, a=4)
            xt_mem = sb("xt", [128, TT * C])
            xt, q16 = four(xt_mem), both(xt_mem)
            qf = sb("qf", [128, TT, C])
            vt_mem = sb("vt", [128, TT * C])
            vt, k16 = four(vt_mem), both(vt_mem)
            v_last = sb("v_last", [128, C])
            kf = sb("kf", [128, TT, C])
            v16 = sb("v16", [128, 2, 2, C], f16)
            spec_v1 = sb("spec_v1", [128, 2, 4, C])
            spec_v = sb("spec_v", [128, 2, 4, C])
            prod_a = sb("prod_a", [128, 4, C])
            prod_b_mem = sb("prod_b", [128, 4 * C])
            prod_b, p16 = four(prod_b_mem), both(prod_b_mem)
            halves = sb("halves", [128, CT, C])
            corr = sb("corr", [128, CT, C])
            top = sb("top", [128, CT, 16])
            neg_max, w_sum, w_inv = sb("neg_max", [128, CT]), sb("w_sum", [128, CT]), sb("w_inv", [128, CT])
            w16 = sb("w16", [128, 2, TT, C], f16)
            spec_w = sb("spec_w", [128, 2, 5, C])
            spec_o = sb("spec_o", [128, 2, 4, C])
            term = sb("term", [128, 3, 2, C])
            xres = sb("xres", [128, TT, C])
            xstat = sb("xstat", [128, TT, C])
            x_stats = sb("x_stats", [128, TT, NCH, 6])
            mv, var, std, tmp = sb("mv", [128, TT, 2]), sb("var", [128, TT]), sb("std", [128, TT]), sb("tmp", [128, TT])
            ln1_scale, ln1_bias = sb("ln1_scale", [128, TT]), sb("ln1_bias", [128, TT])
            v_dc = sb("v_dc", [1, C])
            dc_factor = sb("dc_factor", [1, 128])

            early = [prod_a[:, :, :], halves[:, :, :], corr[:, :, :], xres[:, :, :]]
            front, back = bank[0:3], bank[3:7]

            table16_loaded, table_loaded, dc_factor_set = sem("table16_loaded"), sem("table_loaded"), sem("dc_factor_set")
            x_loaded, v_loaded, v_last_loaded = sem("x_loaded"), sem("v_loaded"), sem("v_last_loaded")
            v_hi_made, v_lo_made, q_hi_made, q_lo_made = sem("v_hi_made"), sem("v_lo_made"), sem("q_hi_made"), sem("q_lo_made")
            p_hi_made, p_lo_made, w_lo_made = sem("p_hi_made"), sem("p_lo_made"), sem("w_lo_made")
            res_loaded, dc_loaded, x2_stored = sem("res_loaded"), sem("dc_loaded"), sem("x2_stored")
            early_loaded = [sem(f"early_loaded{n}") for n in range(NCH)]
            xstat_loaded, xstat_used = sem("xstat_loaded"), sem("xstat_used")
            ln1_var, ln1_sqrt, ln1_ready = sem("ln1_var"), sem("ln1_sqrt"), sem("ln1_ready")
            mv_made, ln1_step = sem("mv_made"), sem("ln1_step")
            x_normed, q_folded, v_shifted, k_folded = sem("x_normed"), sem("q_folded"), sem("v_shifted"), sem("k_folded")
            q_made, q_used, v_made, v_copied = sem("q_made"), sem("q_used"), sem("v_made"), sem("v_copied")
            prod_made, corr_made, halves_copied = sem("prod_made"), sem("corr_made"), sem("halves_copied")
            corr_ready, top_ready, exp_made, w_made, w_scaled = (sem("corr_ready"), sem("top_ready"), sem("exp_made"),
                                                                 sem("w_made"), sem("w_scaled"))
            w_turned, w_copied, wspec_made, wspec_copied = (sem("w_turned"), sem("w_copied"), sem("wspec_made"),
                                                            sem("wspec_copied"))
            term_made, term_added, dc_added, out_made, out_used = (sem("term_made"), sem("term_added"), sem("dc_added"),
                                                                   sem("out_made"), sem("out_used"))
            block = s.enter_context(nc.Block())

            LOOP, TURN = (2, STEPS - 6), NCH

            def least(i):
                return i if isinstance(i, int) else LOOP[0]

            def most(i):
                return i if isinstance(i, int) else LOOP[1] - 1

            def steps(eng, step):
                for i in range(LOOP[0]):
                    step(i, i % 2, i % NCH)
                with eng.Fori(0, (LOOP[1] - LOOP[0]) // TURN) as m:
                    for u in range(LOOP[0], LOOP[0] + TURN):
                        step(TURN * m + u, u % 2, u % NCH)
                for i in range(LOOP[1], STEPS + 1):
                    step(i, i % 2, i % NCH)

            OUT_ORDER = [2, 3, 0, 1]
            W_TABLES = [ER, ERZP, OR, EIZ, OI]
            V_TABLES = [ER, OR, EI, OI]
            Q_TABLES = [ER, EIZ, ERZM, OR, OI]

            @block.sync
            def _(sp):
                def load_v(i):
                    if least(i) >= 1:
                        sp.wait_ge(v_made, 8 * i)
                    b, c = i // NCH, (i % NCH) * C
                    sp.nop(nofuse=True)
                    sp.dma_start(vt, v_t[b, :, :, ds(c, C)]).then_inc(v_loaded, 16)
                    sp.dma_start(v_last[:, :], ctx_v[b, L - 1:L, ds(c, C)].to_broadcast([128, C]))\
                      .then_inc(v_last_loaded, 16)

                def load_x(i):
                    if least(i) >= 1:
                        sp.wait_ge(q_made, 5 * i)
                    b, c = i // NCH, (i % NCH) * C
                    sp.nop(nofuse=True)
                    sp.dma_start(xt, x_t[b, :, :, ds(c, C)]).then_inc(x_loaded, 16)

                def load_res(i):
                    if least(i) >= 1:
                        sp.wait_ge(x2_stored, 16 * i)
                    b, c = i // NCH, (i % NCH) * C
                    sp.nop(nofuse=True)
                    sp.dma_start(xres[:, :, :], x_t[b, :, :, ds(c, C)]).then_inc(res_loaded, 16)
                    sp.dma_start(v_dc[:, :], ctx_v[b, L - 1:L, ds(c, C)]).then_inc(dc_loaded, 16)

                def store(i):
                    sp.wait_ge(out_used, 4 * (i + 1))
                    b, c = i // NCH, (i % NCH) * C
                    sp.nop(nofuse=True)
                    sp.dma_start(x2_t[b, :, :, ds(c, C)], xres[:, :, :]).then_inc(x2_stored, 16)

                def load_stats(n):
                    if least(n) > NCH:
                        sp.wait_ge(xstat_used, n)
                    sp.nop(nofuse=True)
                    b, c = n // NCH, (n % NCH) * C
                    sp.dma_start(xstat[:, :, :], x_t[b, :, :, ds(c, C)]).then_inc(xstat_loaded, 16)

                load_v(0)
                sp.dma_start(table16[:, :], tables16).then_inc(table16_loaded, 16)
                for n in range(NCH):
                    sp.dma_start(early[n], x_t[0, :, :, n * C:(n + 1) * C]).then_inc(early_loaded[n], 16)
                load_x(0)
                sp.dma_start(table[:, :], tables[:, 0:INV]).then_inc(table_loaded, 16)
                sp.dma_start(ident[:, :], tables[:, INV:INV + 128]).then_inc(ident_loaded, 16)
                sp.dma_start(gates_raw[:, 0:1], g_xattn.to_broadcast([128, 1])).then_inc(gates_loaded, 16)
                sp.dma_start(gates_raw[:, 1:2], g_ffn.to_broadcast([128, 1])).then_inc(gates_loaded, 16)
                load_stats(NCH)
                load_v(1)
                b_view = norm[:, :].rearrange("p (n e r) -> p n e r", e=E, r=R)
                for e in range(E):
                    sp.dma_start(b_view[:, :, e, :], b_w[e].rearrange("(n p) r -> p n r", p=128)).then_inc(b_loaded, 16)

                def step(i, par, phase):
                    if most(i) + NCH + 1 < STEPS:
                        load_stats(i + NCH + 1)
                    if most(i) + 1 < STEPS:
                        load_x(i + 1)
                    if least(i) >= 1:
                        load_res(i - 1)
                    if most(i) + 2 < STEPS:
                        load_v(i + 2)
                    if least(i) >= 1:
                        store(i - 1)

                steps(sp, step)
                sp.wait_ge(x2_stored, 16 * STEPS)

            @block.tensor
            def _(pe):
                def times3(to, weights, data, start, stop):
                    pe.matmul(to, weights[0], data[0], start=start, stop=False)
                    pe.matmul(to, weights[0], data[1], start=False, stop=False)
                    return pe.matmul(to, weights[1], data[0], start=False, stop=stop)

                def forward(to, tab, data):
                    for j in range(2):
                        mm = times3(to, [fwd16[:, h, tab, j, :] for h in range(2)], [data(h, j) for h in range(2)],
                                    j == 0, j == 1)
                    return mm

                def v_spectra(i):
                    for n in range(8):
                        if n < 4:
                            if least(i) >= 1:
                                pe.wait_ge(halves_copied, 4 * (i - 1) + n + 1)
                            if n == 0:
                                pe.wait_ge(v_lo_made, 3 * (i + 1))
                        else:
                            pe.wait_ge(v_copied, 8 * i + n - 3)
                        tab = V_TABLES[n % 4]
                        fold = 2 if tab >= OR else 0
                        forward(back[n % 4][:, :], tab,
                                (lambda h, j: k16[:, h, fold + j, :]) if n < 4 else (lambda h, j: v16[:, h, j, :]))\
                            .then_inc(v_made, 1)

                def q_spectra(i, first, last):
                    for n in range(first, last):
                        if n >= 3:
                            pe.wait_ge(q_used, 5 * i + n - 2)
                        elif least(i) >= 2:
                            pe.wait_ge(wspec_copied, 10 * (i - 2) + n + 8)
                        elif i == 1:
                            pe.wait_ge(q_used, 5)
                        if n == 0:
                            pe.wait_ge(q_lo_made, 2 * i + 1)
                        if n == 3:
                            pe.wait_ge(q_lo_made, 2 * i + 2)
                        tab = Q_TABLES[n]
                        fold = 2 if tab >= OR else 0
                        forward(front[n % 3][:, :], tab, lambda h, j: q16[:, h, fold + j, :]).then_inc(q_made, 1)

                def turn_w(c):
                    for j in range(TT):
                        if least(c) >= 1:
                            pe.wait_ge(out_used, 4 * (c - 1) + j + 1)
                        else:
                            pe.wait_ge(v_copied, 8 + 4 + j + 1)
                        for ct in range(CT):
                            if j == 0:
                                pe.wait_ge(w_scaled, 4 * c + ct + 1)
                            mm = pe.transpose(back[j][:, ct * 128:(ct + 1) * 128], corr[:, ct, j * 128:(j + 1) * 128],
                                              ident[:, :])
                        mm.then_inc(w_turned, 1)

                def w_spectra(c):
                    for k in range(10):
                        y, tab = k // 5, W_TABLES[k % 5]
                        if k >= 3:
                            pe.wait_ge(wspec_copied, 10 * c + k - 2)
                        elif most(c) + 1 < STEPS:
                            pe.wait_ge(q_used, 5 * (c + 1) + k + 3)
                        else:
                            pe.wait_ge(wspec_copied, 10 * c)
                        if k % 5 == 0:
                            pe.wait_ge(w_lo_made, 4 * c + 2 * y + 2)
                        forward(front[(5 + k) % 3][:, :], tab, lambda h, j: w16[:, h, 2 * y + j, :]).then_inc(wspec_made, 1)

                def correlate(i):
                    pe.wait_ge(p_lo_made, 2 * (i + 1))
                    for ct in range(CT):
                        if least(i) >= 1:
                            pe.wait_ge(w_lo_made, 4 * (i - 1) + ct + 1)
                        else:
                            pe.wait_ge(v_copied, 4 + ct + 1)
                        for o in range(2):
                            for k in range(2):
                                slot = o + 2 * k
                                mm = times3(back[ct][:, o * HALF:(o + 1) * HALF],
                                            [p16[:, h, slot, ct * 128:(ct + 1) * 128] for h in range(2)],
                                            [inv16[:, h, slot, :] for h in range(2)], k == 0, k == 1)
                        mm.then_inc(corr_made, 1)

                def out_tiles(c):
                    for j in range(TT):
                        if most(c) + 2 < STEPS:
                            pe.wait_ge(v_copied, 8 * (c + 2) + 4 + j + 1)
                        elif c + 2 == STEPS:
                            pe.wait_ge(halves_copied, 4 * (c + 1) + j + 1)
                        else:
                            pe.wait_ge(w_lo_made, 4 * c + j + 1)
                        if j == 0:
                            pe.wait_ge(dc_added, 3 * c + 2)
                        if j == 2:
                            pe.wait_ge(dc_added, 3 * c + 3)
                        h, p = OUT_ORDER[j] // 2, OUT_ORDER[j] % 2
                        for slot in range(4):
                            mm = pe.matmul(back[j][:, :], inv[:, slot, p * 128:(p + 1) * 128], spec_o[:, h, slot, :],
                                           start=(slot == 0), stop=(slot == 3))
                        mm.then_inc(out_made, 1)

                pe.wait_ge(table16_loaded, 16)
                v_spectra(0)
                pe.wait_ge(table_loaded, 16)
                pe.wait_ge(ident_loaded, 16)

                def step(i, par, phase):
                    if most(i) < STEPS:
                        q_spectra(i, 0, 3)
                    if least(i) >= 1:
                        turn_w(i - 1)
                    if most(i) < STEPS:
                        q_spectra(i, 3, 5)
                    if least(i) >= 1:
                        w_spectra(i - 1)
                    if most(i) < STEPS:
                        correlate(i)
                    if most(i) + 1 < STEPS:
                        v_spectra(i + 1)
                    if least(i) >= 1:
                        out_tiles(i - 1)

                steps(pe, step)

            @block.scalar
            def _(act):
                def normalise(i):
                    act.wait_ge(x_loaded, 16 * (i + 1))
                    act.wait_ge(ln1_ready, i // NCH + 1)
                    for t in range(TT):
                        act.activation(xt[:, t, :], xt[:, t, :], ACT.Identity, bias=ln1_bias[:, t:t + 1],
                                       scale=ln1_scale[:, t:t + 1]).then_inc(x_normed, 1)

                def copy_v(i, par):
                    for n in range(8):
                        if n % 4 == 0 and least(i) >= 2:
                            act.wait_ge(term_made, 12 * (i - 2) + (4 if n == 0 else 12))
                        act.wait_ge(v_made, 8 * i + n + 1)
                        to = (spec_v if n < 4 else spec_v1)[:, par, n % 4, :]
                        act.activation(to, back[n % 4][:, :], ACT.Copy, scale=V_SCALE / T_SCALE).then_inc(v_copied, 1)

                def high_v(i, n):
                    if n == 0:
                        act.wait_ge(v_shifted, 4 * i + 2)
                        act.activation(v16[:, 0, :, :], vt[:, 2:4, :], ACT.Copy).then_inc(v_hi_made, 1)
                    else:
                        act.wait_ge(k_folded, 4 * (i + 1))
                        f = 2 * (n - 1)
                        act.activation(k16[:, 0, f:f + 2, :], kf[:, f:f + 2, :], ACT.Copy).then_inc(v_hi_made, 1)

                def high_q(i):
                    act.wait_ge(q_folded, 4 * (i + 1))
                    for f in (0, 2):
                        act.activation(q16[:, 0, f:f + 2, :], qf[:, f:f + 2, :], ACT.Copy).then_inc(q_hi_made, 1)

                def high_p(i):
                    act.wait_ge(prod_made, 2 * (i + 1))
                    for f in (0, 2):
                        act.activation(p16[:, 0, f:f + 2, :], prod_a[:, f:f + 2, :], ACT.Copy).then_inc(p_hi_made, 1)

                def copy_w(c):
                    if least(c) >= 1:
                        act.wait_ge(wspec_made, 10 * c)
                    for j in range(TT):
                        act.wait_ge(w_turned, 4 * c + j + 1)
                        act.activation(w16[:, 0, j, :], back[j][:, :], ACT.Copy).then_inc(w_copied, 1)

                def copy_wspec(c, first, last):
                    if first == 0 and least(c) >= 1:
                        act.wait_ge(term_made, 12 * c)
                    for k in range(first, last):
                        act.wait_ge(wspec_made, 10 * c + k + 1)
                        act.activation(spec_w[:, k // 5, k % 5, :], front[(5 + k) % 3][:, :], ACT.Copy,
                                       scale=1.0 / (V_SCALE * T_SCALE))\
                           .then_inc(wspec_copied, 1)

                def copy_halves(i):
                    if least(i) >= 1:
                        act.wait_ge(w_made, 4 * i)
                    for ct in range(CT):
                        act.wait_ge(corr_made, 4 * i + ct + 1)
                        act.activation(halves[:, ct, :], back[ct][:, :], ACT.Copy, scale=1.0 / T_SCALE).then_inc(halves_copied, 1)

                def exponentials(i):
                    act.wait_ge(top_ready, 1 + 4 * i)
                    for ct in range(CT):
                        act.activation(halves[:, ct, :], corr[:, ct, :], ACT.Exp, bias=neg_max[:, ct:ct + 1])\
                           .then_inc(exp_made, 1)

                def scale_w(i):
                    act.wait_ge(top_ready, 4 * (i + 1))
                    for ct in range(CT):
                        act.activation(corr[:, ct, :], corr[:, ct, :], ACT.Copy, scale=w_inv[:, ct:ct + 1])\
                           .then_inc(w_scaled, 1)

                def deviation(b):
                    act.wait_ge(ln1_var, b + 1)
                    act.activation(std[:, :], var[:, :], ACT.Sqrt).then_inc(ln1_sqrt, 1)

                for n in range(3):
                    high_v(0, n)
                deviation(0)
                copy_v(0, 0)
                normalise(0)
                high_q(0)
                act.wait_ge(gates_loaded, 32)
                act.activation(gates[:, :], gates_raw[:, :], ACT.Tanh).then_inc(gates_ready, 1)

                def step(i, par, phase):
                    if least(i) >= 1:
                        copy_w(i - 1)
                    for n in range(3):
                        if least(i) >= 1:
                            copy_wspec(i - 1, n, n + 1)
                        if most(i) + 1 < STEPS:
                            high_v(i + 1, n)
                    if least(i) >= 1:
                        copy_wspec(i - 1, 3, 5)
                    if most(i) < STEPS:
                        high_p(i)
                    if least(i) >= 1:
                        copy_wspec(i - 1, 5, 10)
                    if most(i) + 1 < STEPS:
                        normalise(i + 1)
                    if phase == NCH - 2 and most(i) + NCH < STEPS:
                        deviation(i // NCH + 1)
                    if most(i) < STEPS:
                        copy_halves(i)
                    if most(i) == 0:
                        high_q(1)
                    if most(i) + 1 < STEPS:
                        copy_v(i + 1, 1 - par)
                    if most(i) < STEPS:
                        exponentials(i)
                    if least(i) >= 1 and most(i) + 1 < STEPS:
                        high_q(i + 1)
                    if most(i) < STEPS:
                        scale_w(i)

                steps(act, step)

            @block.vector
            def _(dve):
                def q_times_k(i, par, first, last):
                    if first == 0:
                        dve.wait_ge(v_copied, 8 * i + 4)
                        if least(i) >= 1:
                            dve.wait_ge(corr_made, 4 * i)
                    k = spec_v[:, par]
                    uses = [[(prod_a, 0, 0)], [(prod_b, 0, 2), (prod_a, 2, 0)], [(prod_b, 2, 2)],
                            [(prod_a, 1, 1), (prod_b, 3, 3)], [(prod_b, 1, 3), (prod_a, 3, 1)]]
                    for n in range(first, last):
                        dve.wait_ge(q_made, 5 * i + n + 1)
                        for to, slot, kslot in uses[n]:
                            op = dve.tensor_tensor(to[:, slot, :], front[n % 3][:, :], k[:, kslot, :], ALU.mult)
                        op.then_inc(q_used, 1)

                def low_w(c):
                    if least(c) >= 1:
                        dve.wait_ge(wspec_made, 10 * c)
                    for j in range(TT):
                        dve.wait_ge(w_copied, 4 * c + j + 1)
                        dve.tensor_tensor(w16[:, 1, j, :], back[j][:, :], w16[:, 0, j, :], ALU.subtract)\
                           .then_inc(w_lo_made, 1)

                def low_v(i):
                    dve.wait_ge(v_hi_made, 3 * i + 1)
                    dve.tensor_tensor(v16[:, 1, :, :], vt[:, 2:4, :], v16[:, 0, :, :], ALU.subtract).then_inc(v_lo_made, 1)
                    dve.wait_ge(v_lo_made, 3 * i + 1)
                    for n, f in enumerate((0, 2)):
                        dve.wait_ge(v_hi_made, 3 * i + n + 2)
                        dve.tensor_tensor(k16[:, 1, f:f + 2, :], kf[:, f:f + 2, :], k16[:, 0, f:f + 2, :], ALU.subtract)\
                           .then_inc(v_lo_made, 1)

                def low_q(i):
                    for n, f in enumerate((0, 2)):
                        dve.wait_ge(q_hi_made, 2 * i + n + 1)
                        dve.tensor_tensor(q16[:, 1, f:f + 2, :], qf[:, f:f + 2, :], q16[:, 0, f:f + 2, :], ALU.subtract)\
                           .then_inc(q_lo_made, 1)

                def low_p(i):
                    for n, f in enumerate((0, 2)):
                        dve.wait_ge(p_hi_made, 2 * i + n + 1)
                        dve.tensor_tensor(p16[:, 1, f:f + 2, :], prod_a[:, f:f + 2, :], p16[:, 0, f:f + 2, :], ALU.subtract)\
                           .then_inc(p_lo_made, 1)

                def v_times_w(c, par, first, last):
                    v1r, v1i = spec_v1[:, par, 0:2, :], spec_v1[:, par, 2:4, :]
                    vr, vi = spec_v[:, par, 0:2, :], spec_v[:, par, 2:4, :]
                    r, rz, im = ([spec_w[:, y, 0:3:2, :] for y in range(2)], [spec_w[:, y, 1:3, :] for y in range(2)],
                                 [spec_w[:, y, 3:5, :] for y in range(2)])
                    o1r, o1i, o0r, o0i = spec_o[:, 1, 0:2, :], spec_o[:, 1, 2:4, :], spec_o[:, 0, 0:2, :], spec_o[:, 0, 2:4, :]
                    todo = [(o0r, vr, r[0]), (None, vi, im[0]), (o0i, vi, rz[0]), (None, vr, im[0]),
                            (o1r, v1r, r[0]), (None, v1i, im[0]), (o1i, v1i, rz[0]), (None, v1r, im[0]),
                            (None, v1r, r[1]), (None, v1i, rz[1]), (None, v1i, im[1]), (None, v1r, im[1])]
                    if first == 0:
                        if least(c) >= 1:
                            dve.wait_ge(out_made, 4 * c)
                            dve.wait_ge(term_added, 8 * c)
                        dve.wait_ge(wspec_copied, 10 * c + 5)
                    t = sum(to is None for to, _, _ in todo[:first])
                    for n, (to, a, w) in list(enumerate(todo))[first:last]:
                        if n == 8:
                            dve.wait_ge(wspec_copied, 10 * c + 10)
                        if to is None:
                            if t >= 3:
                                dve.wait_ge(term_added, 8 * c + t - 2)
                            to = term[:, t % 3]
                            t += 1
                        dve.tensor_tensor(to, a, w, ALU.mult).then_inc(term_made, 1)

                def largest(i):
                    if least(i) >= 1:
                        dve.wait_ge(w_turned, 4 * i)
                    dve.wait_ge(p_lo_made, 2 * (i + 1))
                    for ct in range(CT):
                        e, o = halves[:, ct, 0:HALF], halves[:, ct, HALF:C]
                        dve.wait_ge(halves_copied, 4 * i + ct + 1)
                        dve.tensor_tensor(corr[:, ct, 0:HALF], e, o, ALU.add).then_inc(corr_ready, 1)
                        dve.tensor_tensor(corr[:, ct, HALF:C], e, o, ALU.subtract).then_inc(corr_ready, 1)
                    base = 20 * i
                    for ct in range(CT):
                        dve.wait_ge(corr_ready, base + 2 * ct + 2)
                        dve.nop(nofuse=True)
                        dve.max(top[:, ct, 0:8], corr[:, ct, :]).then_inc(corr_ready, 1)
                    dve.wait_ge(corr_ready, base + 12)
                    dve.tensor_scalar(neg_max[:, :], top[:, :, 0], -1.0, None, ALU.mult).then_inc(top_ready, 1)
                    for ct in range(CT):
                        dve.match_replace(prod_a[:, ct, :], top[:, ct, 0:8], corr[:, ct, :], -3.0e38)\
                           .then_inc(corr_ready, 1)
                    for ct in range(CT):
                        dve.wait_ge(corr_ready, base + 12 + ct + 1)
                        dve.nop(nofuse=True)
                        dve.max(top[:, ct, 8:16], prod_a[:, ct, :]).then_inc(corr_ready, 1)
                def select(i):
                    for ct in range(CT):
                        dve.wait_ge(corr_ready, 20 * i + 16 + ct + 1)
                        dve.wait_ge(exp_made, 4 * i + ct + 1)
                        dve.scalar_tensor_tensor(out=corr[:, ct, :], in0=corr[:, ct, :], scalar=top[:, ct, TOPK - 1:TOPK],
                                                 in1=halves[:, ct, :], op0=ALU.is_ge, op1=ALU.mult,
                                                 accum_out=w_sum[:, ct:ct + 1]).then_inc(w_made, 1)
                    dve.wait_ge(w_made, 4 * (i + 1))
                    dve.reciprocal(w_inv[:, :], w_sum[:, :]).then_inc(top_ready, 3)

                def residual(c):
                    dve.wait_ge(res_loaded, 16 * (c + 1))
                    for j in range(TT):
                        t = OUT_ORDER[j]
                        dve.wait_ge(out_made, 4 * c + j + 1)
                        dve.scalar_tensor_tensor(out=xres[:, t, :], in0=back[j][:, :], scalar=gates[:, 0:1],
                                                 in1=xres[:, t, :], op0=ALU.mult, op1=ALU.add).then_inc(out_used, 1)

                def take_stats(n, chunk, early_from=None):
                    if early_from is not None:
                        dve.wait_ge(early_loaded[chunk], 16)
                    else:
                        dve.wait_ge(xstat_loaded, 16 * (n - NCH + 1))
                    x_from = xstat[:, :, :] if early_from is None else early_from
                    for t in range(TT):
                        op = dve.bn_stats(x_stats[:, t, chunk, :], x_from[:, t, :])
                    op.then_inc(xstat_used, 1)

                def variance(b):
                    dve.wait_ge(xstat_used, NCH * (b + 1))
                    dve.nop(nofuse=True)
                    for t in range(TT):
                        op = dve.bn_aggr(mv[:, t, :], x_stats[:, t, :, :].rearrange("p a b -> p (a b)"))
                    op.then_inc(mv_made, 1)
                    dve.wait_ge(mv_made, b + 1)
                    dve.tensor_scalar(var[:, :], mv[:, :, 1], EPS, None, ALU.add).then_inc(ln1_var, 1)

                def scales(b):
                    newton(dve, ln1_step, 6 * b, ln1_sqrt, b + 1, var, std, tmp, mv[:, :, 0], ln1_scale, ln1_bias, 1.0)
                    dve.wait_ge(ln1_step, 6 * (b + 1))
                    dve.tensor_copy(tmp[:, :], ln1_bias[:, :]).then_inc(ln1_ready, 1)

                def step(i, par, phase):
                    if most(i) < STEPS:
                        q_times_k(i, par, 0, 3)
                    if least(i) >= 1:
                        low_w(i - 1)
                    if most(i) < STEPS:
                        q_times_k(i, par, 3, 5)
                    more = most(i) + NCH + 1 < STEPS
                    if more:
                        take_stats(i + NCH + 1, (phase + 1) % NCH)
                    if more and phase == NCH - 2:
                        variance(i // NCH + 1)
                    if most(i) + 1 < STEPS:
                        low_v(i + 1)
                    if least(i) >= 1:
                        v_times_w(i - 1, 1 - par, 0, 2)
                    if most(i) < STEPS:
                        low_p(i)
                    if least(i) >= 1:
                        v_times_w(i - 1, 1 - par, 2, 12)
                    if most(i) == 0:
                        low_q(1)
                    if most(i) < STEPS:
                        largest(i)
                        select(i)
                    if least(i) >= 1 and most(i) + 1 < STEPS:
                        low_q(i + 1)
                    if least(i) >= 1:
                        residual(i - 1)
                    if more and phase == NCH - 2:
                        dve.wait_ge(x_normed, 4 * (i + 2))
                        scales(i // NCH + 1)

                for n in range(NCH):
                    if n == 2:
                        low_v(0)
                    take_stats(n, n, early[n])
                variance(0)
                scales(0)
                low_q(0)
                dve.wait_ge(gates_ready, 1)
                take_stats(NCH, 0)
                steps(dve, step)

            @block.gpsimd
            def _(pool):
                def prepare_v(i):
                    pool.wait_ge(v_loaded, 16 * (i + 1))
                    pool.wait_ge(v_last_loaded, 16 * (i + 1))
                    if least(i) >= 1:
                        pool.wait_ge(v_lo_made, 3 * i)
                    for t in (2, 3, 0, 1):
                        pool.tensor_tensor(vt[:, t, :], vt[:, t, :], v_last[:, :], ALU.subtract)\
                            .then_inc(v_shifted, 1)
                    pool.wait_ge(v_shifted, 4 * (i + 1))
                    for j in range(4):
                        pool.tensor_tensor(kf[:, j, :], vt[:, j % 2, :], vt[:, 2 + j % 2, :],
                                           ALU.add if j < 2 else ALU.subtract).then_inc(k_folded, 1)

                def fold_q(i):
                    if least(i) >= 1:
                        pool.wait_ge(q_lo_made, 2 * i)
                    pool.wait_ge(x_normed, 4 * (i + 1))
                    for j in range(4):
                        pool.tensor_tensor(qf[:, j, :], xt[:, j % 2, :], xt[:, 2 + j % 2, :],
                                           ALU.add if j < 2 else ALU.subtract).then_inc(q_folded, 1)

                def sum_qk(i):
                    pool.wait_ge(q_used, 5 * (i + 1))
                    pool.tensor_tensor(prod_a[:, 0:2, :], prod_a[:, 0:2, :], prod_b[:, 0:2, :], ALU.add)\
                        .then_inc(prod_made, 1)
                    pool.tensor_tensor(prod_a[:, 2:4, :], prod_a[:, 2:4, :], prod_b[:, 2:4, :], ALU.subtract)\
                        .then_inc(prod_made, 1)

                def sum_vw(c):
                    o1r, o1i, o0r, o0i = spec_o[:, 1, 0:2, :], spec_o[:, 1, 2:4, :], spec_o[:, 0, 0:2, :], spec_o[:, 0, 2:4, :]
                    todo = [(o0r, ALU.add, 2, 0), (o0i, ALU.subtract, 4, 0), (o1r, ALU.add, 6, 0),
                            (o1i, ALU.subtract, 8, 0), (o0r, ALU.add, 9, 1), (o0i, ALU.add, 10, 2),
                            (o0r, ALU.add, 11, 5), (o0i, ALU.subtract, 12, 6)]
                    pool.wait_ge(dc_loaded, 16 * (c + 1))
                    dc_row = v_dc[:, :].rearrange("p (a c) -> p a c", c=128)
                    pool.tensor_tensor(dc_row, dc_row, dc_factor[:, :].rearrange("p (a c) -> p a c", a=1).to_broadcast([1, CT, 128]),
                                       ALU.mult).then_inc(dc_added, 1)
                    dc_at = {3: 1, 7: 0}
                    for t, (to, sign, made, own) in enumerate(todo):
                        pool.wait_ge(term_made, 12 * c + made)
                        if own:
                            pool.wait_ge(term_added, 8 * c + own)
                        pool.tensor_tensor(to, to, term[:, t % 3], sign).then_inc(term_added, 1)
                        if t in dc_at:
                            if t == 3:
                                pool.wait_ge(dc_added, 3 * c + 1)
                            pool.wait_ge(term_added, 8 * c + t + 1)
                            dc = spec_o[0:1, dc_at[t], 0, :]
                            pool.tensor_tensor(dc, dc, v_dc[:, :], ALU.add).then_inc(dc_added, 1)

                pool.memset(dc_factor[:, :], float(L)).then_inc(dc_factor_set, 1)
                pool.wait_ge(dc_factor_set, 1)
                prepare_v(0)
                fold_q(0)

                def step(i, par, phase):
                    if most(i) + 1 < STEPS:
                        prepare_v(i + 1)
                    if most(i) < STEPS:
                        sum_qk(i)
                    if least(i) >= 1:
                        sum_vw(i - 1)
                    if most(i) + 1 < STEPS:
                        fold_q(i + 1)

                steps(pool, step)

        with ExitStack() as s:
            def sb(name, shape, dt=f32):
                return s.enter_context(nc.sbuf_tensor(name, shape, dt))

            w_hi, w_lo = sb("w_hi", [128, KD, D], f16), sb("w_lo", [128, KD, D], f16)
            ag_hi, ag_lo = sb("ag_hi", [128, KD, NG], f16), sb("ag_lo", [128, KD, NG], f16)
            b_hi, b_lo = sb("b_hi", [128, D], f16), sb("b_lo", [128, D], f16)
            row = sb("row", [128, 2, D])
            wrow = sb("wrow", [128, 2, D])
            nt_hi, nt_lo = sb("nt_hi", [128, KD, 128], f16), sb("nt_lo", [128, KD, 128], f16)
            bias = sb("bias", [128, D])
            ln2_scale, ln2_bias = sb("ln2_scale", [128, 1]), sb("ln2_bias", [128, 1])
            stats, mv = sb("stats2", [128, NCH, 6]), sb("mv2", [128, 2])
            var, std, tmp = sb("var2", [128, 1]), sb("std2", [128, 1]), sb("tmp2", [128, 1])
            thr_b, out_gate = sb("thr_b", [128, 1]), sb("out_gate", [128, 1])
            logit = sb("logit", [128, NG])
            lmax, esum, erec, wsum, wzero = (sb(n, [128, 1]) for n in ("lmax", "esum", "erec", "wsum", "wzero"))
            thr = sb("thr", [128, 1])
            gate = sb("gate", [128, E])
            hw = sb("hw", [128, E * R])
            hwt_hi, hwt_lo = sb("hwt_hi", [128, 128], f16), sb("hwt_lo", [128, 128], f16)

            row_loaded = [sem(f"row_loaded{n}") for n in range(4)]
            small_loaded = sem("small_loaded")
            wt_made, wt_hi, wt_lo = sem("wt_made"), sem("wt_hi"), sem("wt_lo")
            ln2_step, ln2_sqrt, bias_ready = sem("ln2_step"), sem("ln2_sqrt"), sem("bias_ready")

            NW = D // 128
            JOBS = NW + 2
            DESCALE = 1.0 / (N_SCALE * W_SCALE)

            def weight_row(n):
                return (row if n % 4 < 2 else wrow)[:, n % 2, :]

            def weight_target(n, q, part):
                if n < NW:
                    return (w_hi, w_lo)[part][:, 4 * q:4 * q + 4, n * 128:(n + 1) * 128]
                t = (ag_hi, ag_lo)[part]
                return t[:, 4 * q:4 * q + 4, 0:128] if n == NW else t[:, 4 * q:4 * q + 4, 128:NG]

            def weight_bank(n, q):
                cols = 128 if n <= NW else E + 1
                view = bank[(4 * n + q) % 8][:, 0:4 * cols] if cols == 128 else bank[(4 * n + q) % 8][:, 0:4 * 16]
                view = view.rearrange("p (k c) -> p k c", k=4)
                return view if cols == 128 else view[:, :, 0:cols]

            with nc.Block() as block:
                @block.sync
                def _(sp):
                    for n in range(JOBS):
                        if n >= 4:
                            sp.wait_ge(wt_made, 4 * (n - 3))
                        to, loaded = weight_row(n), row_loaded[n % 4]
                        if n < NW:
                            sp.dma_start(to, w_base[n * 128:(n + 1) * 128, :]).then_inc(loaded, 16)
                        elif n == NW:
                            sp.dma_start(to, a_w.rearrange("e r d -> (e r) d")).then_inc(loaded, 16)
                        else:
                            sp.dma_start(to[0:E, :], w_gate).then_inc(loaded, 16)
                            sp.dma_start(to[E:E + 1, :], w_thr.rearrange("(a n) -> a n", a=1)).then_inc(loaded, 16)
                    sp.dma_start(bias[:, :], b_base.rearrange("(a n) -> a n", a=1).to_broadcast([128, D])).then_inc(small_loaded, 16)
                    sp.dma_start(thr_b[:, :], b_thr.to_broadcast([128, 1])).then_inc(small_loaded, 16)

                @block.tensor
                def _(pe):
                    for n in range(JOBS):
                        pe.wait_ge(row_loaded[n % 4], 16 * (n // 4 + 1) + (16 if n == JOBS - 1 else 0))
                        rows = 128 if n <= NW else E + 1
                        for q in range(4):
                            if 4 * n + q >= 8:
                                pe.wait_ge(wt_hi, 4 * n + q - 7)
                                pe.wait_ge(wt_lo, 4 * n + q - 7)
                            view = weight_bank(n, q)
                            for k in range(4):
                                d = (4 * q + k) * 128
                                mm = pe.transpose(view[:, k, :], weight_row(n)[0:rows, d:d + 128], ident[0:rows, 0:rows])
                            mm.then_inc(wt_made, 1)
                    pe.wait_ge(b_loaded, 16 * E)
                    for q in range(4):
                        g = 4 * JOBS + q
                        pe.wait_ge(wt_hi, g - 7)
                        pe.wait_ge(wt_lo, g - 7)
                        for k in range(4):
                            mm = pe.transpose(bank[g % 8][:, k * 128:(k + 1) * 128], norm[:, (4 * q + k) * 128:(4 * q + k + 1) * 128],
                                              ident[:, :])
                        mm.then_inc(wt_made, 1)

                @block.scalar
                def _(act):
                    for g in range(4 * JOBS + 4):
                        act.wait_ge(wt_made, g + 1)
                        if g < 4 * JOBS:
                            to, view = weight_target(g // 4, g % 4, 0), weight_bank(g // 4, g % 4)
                        else:
                            q = g - 4 * JOBS
                            to, view = b_hi[:, q * 512:(q + 1) * 512], bank[g % 8][:, :]
                        act.activation(to, view, ACT.Copy, scale=W_SCALE).then_inc(wt_hi, 1)

                @block.vector
                def _(dve):
                    for g in range(4 * JOBS + 4):
                        dve.wait_ge(wt_hi, g + 1)
                        if g < 4 * JOBS:
                            hi, lo, view = (weight_target(g // 4, g % 4, 0), weight_target(g // 4, g % 4, 1),
                                            weight_bank(g // 4, g % 4))
                        else:
                            q = g - 4 * JOBS
                            hi, lo, view = b_hi[:, q * 512:(q + 1) * 512], b_lo[:, q * 512:(q + 1) * 512], bank[g % 8][:, :]
                        dve.scalar_tensor_tensor(out=lo, in0=view, scalar=W_SCALE, in1=hi, op0=ALU.mult, op1=ALU.subtract)\
                           .then_inc(wt_lo, 1)
                    dve.wait_ge(small_loaded, 32)
                    dve.tensor_scalar(bias[:, :], bias[:, :], gates[:, 1:2], None, ALU.mult).then_inc(bias_ready, 1)
                    dve.tensor_scalar(out_gate[:, :], gates[:, 1:2], DESCALE, None, ALU.mult).then_inc(bias_ready, 1)
                    dve.tensor_scalar(thr_b[:, :], thr_b[:, :], -1.0, None, ALU.mult).then_inc(bias_ready, 1)

            x2_loaded = [sem("x2_loaded0"), sem("x2_loaded1")]
            out_stored = [sem("out_stored0"), sem("out_stored1")]
            normed, turned, nt_hi_made, nt_lo_made = sem("normed"), sem("turned"), sem("nt_hi_made"), sem("nt_lo_made")
            logits_made, logits_copied, exps_made, gate_step = (sem("logits_made"), sem("logits_copied"),
                                                                sem("exps_made"), sem("gate_step"))
            hw_turned, hwt_hi_made, hwt_lo_made = sem("hw_turned"), sem("hwt_hi_made"), sem("hwt_lo_made")
            base_made = sem("base_made")
            bias_added, dense_made, out_ready = sem("bias_added"), sem("dense_made"), sem("out_ready")
            dense, turn_bank, logit_bank, hw_bank = bank[0:4], bank[4:6], bank[6], bank[7]
            GATE_OPS, LN2_OPS = 11, 9

            FLOOP = (2, ROWS - 2)

            def fleast(i):
                return i if isinstance(i, int) else FLOOP[0]

            def fmost(i):
                return i if isinstance(i, int) else FLOOP[1] - 1

            def tiles(eng, step):
                for i in range(FLOOP[0]):
                    step(i, i % 2)
                with eng.Fori(0, (FLOOP[1] - FLOOP[0]) // 2) as m:
                    for u in range(2):
                        step(2 * m + (FLOOP[0] + u), u)
                for i in range(FLOOP[1], ROWS):
                    step(i, i % 2)

            with nc.Block() as block:
                @block.sync
                def _(sp):
                    def load(i, par):
                        if fleast(i) >= 2:
                            sp.wait_ge(out_stored[par], 16 * (i // 2))
                        sp.nop(nofuse=True)
                        sp.dma_start(row[:, par, :], x2_rows[i]).then_inc(x2_loaded[par], 16)

                    def step(i, par):
                        if fmost(i) + 1 < ROWS:
                            load(i + 1, 1 - par)
                        sp.wait_ge(out_ready, 4 * (i + 1))
                        sp.nop(nofuse=True)
                        sp.dma_start(out_rows[i], row[:, par, :]).then_inc(out_stored[par], 16)

                    load(0, 0)
                    tiles(sp, step)
                    for par in range(2):
                        sp.wait_ge(out_stored[par], 16 * ROWS // 2)

                @block.tensor
                def _(pe):
                    def turn(i):
                        pe.wait_ge(normed, i + 1)
                        for q in range(4):
                            if q >= 2 or fleast(i) >= 1:
                                pe.wait_ge(nt_hi_made, 4 * i + q - 1)
                                pe.wait_ge(nt_lo_made, 4 * i + q - 1)
                            for k in range(4):
                                d = (4 * q + k) * 128
                                mm = pe.transpose(turn_bank[q % 2][:, k * 128:(k + 1) * 128], norm[:, d:d + 128], ident[:, :])
                            mm.then_inc(turned, 1)

                    def logits(i):
                        if fleast(i) >= 1:
                            pe.wait_ge(logits_copied, i)
                        pe.wait_ge(nt_hi_made, 4 * (i + 1))
                        pe.wait_ge(nt_lo_made, 4 * (i + 1))
                        acc = logit_bank[:, 0:NG]
                        for k in range(KD):
                            pe.matmul(acc, nt_hi[:, k, :], ag_hi[:, k, :], start=(k == 0), stop=False)
                            pe.matmul(acc, nt_hi[:, k, :], ag_lo[:, k, :], start=False, stop=False)
                            mm = pe.matmul(acc, nt_lo[:, k, :], ag_hi[:, k, :], start=False, stop=(k == KD - 1))
                        mm.then_inc(logits_made, 1)

                    def base(i):
                        for k in range(KD):
                            for n, (a, w) in enumerate(((nt_hi, w_hi), (nt_hi, w_lo), (nt_lo, w_hi))):
                                for o in range(4):
                                    if k == 0 and n == 0 and fleast(i) >= 1:
                                        pe.wait_ge(out_ready, 4 * (i - 1) + o + 1)
                                    mm = pe.matmul(dense[o][:, :], a[:, k, :], w[:, k, o * 512:(o + 1) * 512],
                                                   start=(k == 0 and n == 0), stop=False)
                        mm.then_inc(base_made, 1)

                    def turn_hw(i):
                        pe.wait_ge(gate_step, GATE_OPS * (i + 1))
                        if fleast(i) >= 1:
                            pe.wait_ge(hwt_lo_made, i)
                        pe.transpose(hw_bank[:, 0:128], hw[:, :], ident[:, :]).then_inc(hw_turned, 1)

                    def experts(i):
                        pe.wait_ge(hwt_hi_made, i + 1)
                        pe.wait_ge(hwt_lo_made, i + 1)
                        for o in range(4):
                            cols = slice(o * 512, (o + 1) * 512)
                            pe.matmul(dense[o][:, :], hwt_hi[:, :], b_hi[:, cols], start=False, stop=False)
                            pe.matmul(dense[o][:, :], hwt_hi[:, :], b_lo[:, cols], start=False, stop=False)
                            pe.matmul(dense[o][:, :], hwt_lo[:, :], b_hi[:, cols], start=False, stop=True)\
                              .then_inc(dense_made, 1)

                    def step(i, par):
                        logits(i)
                        base(i)
                        turn_hw(i)
                        if fmost(i) + 1 < ROWS:
                            turn(i + 1)
                        experts(i)

                    turn(0)
                    tiles(pe, step)

                @block.scalar
                def _(act):
                    def normalise(i, par):
                        act.wait_ge(ln2_step, LN2_OPS * i + 3)
                        act.activation(std[:, :], var[:, :], ACT.Sqrt).then_inc(ln2_sqrt, 1)
                        act.wait_ge(ln2_step, LN2_OPS * (i + 1))
                        if fleast(i) >= 1:
                            act.wait_ge(turned, 4 * i)
                        act.activation(norm[:, :], row[:, par, :], ACT.Identity, bias=ln2_bias[:, :],
                                       scale=ln2_scale[:, :]).then_inc(normed, 1)

                    def turned_hi(i):
                        if fleast(i) >= 1:
                            act.wait_ge(base_made, i)
                        for q in range(4):
                            act.wait_ge(turned, 4 * i + q + 1)
                            act.activation(nt_hi[:, 4 * q:4 * q + 4, :].rearrange("p k t -> p (k t)"),
                                           turn_bank[q % 2][:, :], ACT.Copy).then_inc(nt_hi_made, 1)

                    def gating(i):
                        act.wait_ge(logits_made, i + 1)
                        if fleast(i) >= 1:
                            act.wait_ge(gate_step, GATE_OPS * i)
                        act.activation(logit[:, :], logit_bank[:, 0:NG], ACT.Copy, scale=DESCALE)\
                           .then_inc(logits_copied, 1)
                        act.wait_ge(gate_step, GATE_OPS * i + 1)
                        act.wait_ge(logits_copied, i + 1)
                        act.activation(gate[:, :], logit[:, E * R:E * R + E], ACT.Exp, bias=lmax[:, :],
                                       accum_out=esum[:, :]).then_inc(exps_made, 1)
                        act.activation(thr[:, :], logit[:, E * R + E:NG], ACT.Exp, bias=thr_b[:, :], scale=-1.0)\
                           .then_inc(exps_made, 1)

                    def hw_hi(i):
                        if fleast(i) >= 1:
                            act.wait_ge(dense_made, 4 * i)
                        act.wait_ge(hw_turned, i + 1)
                        act.activation(hwt_hi[:, :], hw_bank[:, 0:128], ACT.Copy).then_inc(hwt_hi_made, 1)

                    def step(i, par):
                        gating(i)
                        if fmost(i) + 1 < ROWS:
                            normalise(i + 1, 1 - par)
                        hw_hi(i)
                        if fmost(i) + 1 < ROWS:
                            turned_hi(i + 1)

                    normalise(0, 0)
                    turned_hi(0)
                    tiles(act, step)

                @block.vector
                def _(dve):
                    def statistics(i, par):
                        dve.wait_ge(x2_loaded[par], 16 * (i // 2 + 1))
                        for q in range(NCH):
                            op = dve.bn_stats(stats[:, q, :], row[:, par, q * C:(q + 1) * C])
                        op.then_inc(ln2_step, 1)
                        dve.wait_ge(ln2_step, LN2_OPS * i + 1)
                        dve.nop(nofuse=True)
                        dve.bn_aggr(mv[:, :], stats[:, :, :].rearrange("p a b -> p (a b)")).then_inc(ln2_step, 1)
                        dve.wait_ge(ln2_step, LN2_OPS * i + 2)
                        dve.tensor_scalar(var[:, :], mv[:, 1:2], EPS, None, ALU.add).then_inc(ln2_step, 1)
                        if fleast(i) >= 1:
                            dve.wait_ge(normed, i)
                        newton(dve, ln2_step, LN2_OPS * i + 3, ln2_sqrt, i + 1, var, std, tmp, mv[:, 0:1],
                               ln2_scale, ln2_bias, N_SCALE)

                    def turned_lo(i):
                        if fleast(i) >= 1:
                            dve.wait_ge(base_made, i)
                        for q in range(4):
                            dve.wait_ge(nt_hi_made, 4 * i + q + 1)
                            dve.tensor_tensor(nt_lo[:, 4 * q:4 * q + 4, :].rearrange("p k t -> p (k t)"),
                                              turn_bank[q % 2][:, :],
                                              nt_hi[:, 4 * q:4 * q + 4, :].rearrange("p k t -> p (k t)"),
                                              ALU.subtract).then_inc(nt_lo_made, 1)

                    def gating(i):
                        done = [0]

                        def chain(op):
                            op.then_inc(gate_step, 1)
                            done[0] += 1
                            if done[0] < GATE_OPS:
                                dve.wait_ge(gate_step, GATE_OPS * i + done[0])

                        dve.wait_ge(logits_copied, i + 1)
                        chain(dve.tensor_reduce(lmax[:, :], logit[:, E * R:E * R + E], AX.X, ALU.max, negate=True))
                        dve.wait_ge(exps_made, 2 * (i + 1))
                        chain(dve.reciprocal(erec[:, :], esum[:, :]))
                        chain(dve.tensor_scalar(thr[:, :], thr[:, :], 1.0, 1.0 / MAX_THRESHOLD, ALU.add, ALU.mult))
                        chain(dve.reciprocal(thr[:, :], thr[:, :]))
                        chain(dve.tensor_scalar(gate[:, :], gate[:, :], erec[:, :], thr[:, :], ALU.mult, ALU.subtract))
                        chain(dve.tensor_scalar(gate[:, :], gate[:, :], 0.0, None, ALU.max, ALU.add, accum_out=wsum[:, :]))
                        chain(dve.tensor_scalar(wzero[:, :], wsum[:, :], 0.0, None, ALU.is_equal))
                        chain(dve.tensor_tensor(wsum[:, :], wsum[:, :], wzero[:, :], ALU.add))
                        chain(dve.reciprocal(wsum[:, :], wsum[:, :]))
                        chain(dve.tensor_scalar(gate[:, :], gate[:, :], wsum[:, :], SCALING * N_SCALE, ALU.mult, ALU.mult))
                        if fleast(i) >= 1:
                            dve.wait_ge(hw_turned, i)
                        chain(dve.tensor_tensor(hw[:, :].rearrange("p (e r) -> p e r", e=E),
                                                logit[:, 0:E * R].rearrange("p (e r) -> p e r", e=E),
                                                gate[:, :].rearrange("p (e r) -> p e r", r=1).to_broadcast([128, E, R]),
                                                ALU.mult))

                    def hw_lo(i):
                        if fleast(i) >= 1:
                            dve.wait_ge(dense_made, 4 * i)
                        dve.wait_ge(hwt_hi_made, i + 1)
                        dve.tensor_tensor(hwt_lo[:, :], hw_bank[:, 0:128], hwt_hi[:, :], ALU.subtract).then_inc(hwt_lo_made, 1)

                    def finish(i, par):
                        dve.wait_ge(bias_added, i + 1)
                        for o in range(4):
                            cols = slice(o * 512, (o + 1) * 512)
                            dve.wait_ge(dense_made, 4 * i + o + 1)
                            dve.scalar_tensor_tensor(out=row[:, par, cols], in0=dense[o][:, :], scalar=out_gate[:, :],
                                                     in1=row[:, par, cols], op0=ALU.mult, op1=ALU.add).then_inc(out_ready, 1)

                    def step(i, par):
                        gating(i)
                        if fmost(i) + 1 < ROWS:
                            statistics(i + 1, 1 - par)
                        hw_lo(i)
                        if fmost(i) + 1 < ROWS:
                            turned_lo(i + 1)
                        finish(i, par)

                    statistics(0, 0)
                    turned_lo(0)
                    tiles(dve, step)

                @block.gpsimd
                def _(pool):
                    def step(i, par):
                        pool.wait_ge(normed, i + 1)
                        pool.tensor_tensor(row[:, par, :], row[:, par, :], bias[:, :], ALU.add).then_inc(bias_added, 1)

                    pool.wait_ge(bias_ready, 3)
                    tiles(pool, step)


_INS = ['x', 'ctx_4096', 'g_xattn', 'g_ffn', 'L0_ffn_W_base', 'L0_ffn_b_base', 'L0_ffn_W_gate', 'L0_ffn_W_thr',
        'L0_ffn_b_thr', 'L0_ffn_A_w', 'L0_ffn_B_w']


def kernel(**inputs):
    import concourse.bacc as _bacc
    from concourse.bass_utils import run_bass_kernel_spmd as _run

    nc = _bacc.Bacc("TRN2", target_bir_lowering=False, num_devices=1)
    arrays, args = {}, []
    for name, a in [(n, inputs[n]) for n in _INS] + list(zip(("tables", "tables16"), dft_tables())):
        a = np.ascontiguousarray(a)
        arrays[f"in_{name}_dram"] = a
        args.append(nc.dram_tensor(f"in_{name}_dram", a.shape, mybir.dt.from_np(a.dtype), kind="ExternalInput").ap())
    out = nc.dram_tensor("out_0_dram", (B, L, D), mybir.dt.float32, kind="ExternalOutput").ap()
    flamingo_kernel(nc, *args, out)
    r = _run(nc, [arrays], core_ids=[0])
    return r.results[0]["out_0_dram"]
```

```python
import concourse.bass as bass
from concourse import mybir
from contextlib import ExitStack
import numpy as np

B, L, D = 8, 512, 2048
C = 512
HALF = L // 2
TT = L // 128
NCH = D // C
STEPS = B * NCH
CT = C // 128
TOPK = int(2 * np.log(L))
EPS = 1e-5
ROWS = B * L // 128
E, R = 8, 16
KD = D // 128
NG = E * R + E + 1
SCALING = 2.0
MAX_THRESHOLD = 0.125
N_SCALE, W_SCALE = 16.0, 64.0

ER, EI, EIZ, ERZM, OR, OI = range(6)
FWD = 6 * 2 * 128
INV = 4 * HALF
T_SCALE = 16.0
P_SCALE = 1.0 / L
V_SCALE = P_SCALE / T_SCALE


def split16(a):
    hi = a.astype(np.float16)
    return np.stack([hi, (a - hi).astype(np.float16)], axis=1)


def dft_tables():
    t = np.arange(HALF)[:, None].astype(np.float64)
    g = np.arange(128)[None, :].astype(np.float64)
    even, odd = 2 * np.pi * g * t / HALF, 2 * np.pi * (2 * g + 1) * t / L
    nyquist = np.cos(np.pi * t[:, 0])
    er, eiz, o_r, oi = np.cos(even), -np.sin(even), np.cos(odd), -np.sin(odd)
    ei, erzm = eiz.copy(), er.copy()
    ei[:, 0], erzm[:, 0] = nyquist, -nyquist
    fwd = np.stack([er, ei, eiz, erzm, o_r, oi])
    fwd = fwd.reshape(6, 2, 128, 128).transpose(2, 0, 1, 3).reshape(128, FWD)
    ier, iei, ior, ioi = 2 * er.T / L, 2 * eiz.T / L, 2 * o_r.T / L, 2 * oi.T / L
    ier[0] /= 2
    iei[0] = nyquist / L
    inv = np.stack([ier, ior, iei, ioi], axis=1).reshape(128, INV)
    exact = np.concatenate([inv, np.eye(128)], axis=1).astype(np.float32)
    halves = np.concatenate([split16(fwd * T_SCALE).reshape(128, -1), split16(inv * (L * T_SCALE)).reshape(128, -1)], axis=1)
    return exact, halves




def newton(dve, step, done, sqrt_done, sqrt_n, var, std, tmp, mean, scale, bias, factor):
    ALU = mybir.AluOpType
    dve.wait_ge(sqrt_done, sqrt_n)
    dve.reciprocal(scale[:, :], std[:, :]).then_inc(step, 1)
    dve.wait_ge(step, done + 1)
    dve.tensor_tensor(tmp[:, :], scale[:, :], scale[:, :], ALU.mult).then_inc(step, 1)
    dve.wait_ge(step, done + 2)
    dve.tensor_tensor(tmp[:, :], tmp[:, :], var[:, :], ALU.mult).then_inc(step, 1)
    dve.wait_ge(step, done + 3)
    dve.tensor_scalar(tmp[:, :], tmp[:, :], -0.5 * factor, 1.5 * factor, ALU.mult, ALU.add).then_inc(step, 1)
    dve.wait_ge(step, done + 4)
    dve.tensor_tensor(scale[:, :], scale[:, :], tmp[:, :], ALU.mult).then_inc(step, 1)
    dve.wait_ge(step, done + 5)
    dve.scalar_tensor_tensor(out=bias[:, :], in0=mean, scalar=-1.0, in1=scale[:, :],
                             op0=ALU.mult, op1=ALU.mult).then_inc(step, 1)


def flamingo_kernel(nc, x, ctx_v, g_xattn, g_ffn, w_base, b_base, w_gate, w_thr, b_thr, a_w, b_w,
                    tables, tables16, out):
    f32, f16 = mybir.dt.float32, mybir.dt.float16
    ALU, ACT, AX = mybir.AluOpType, mybir.ActivationFunctionType, mybir.AxisListType
    ds = bass.ds

    x2 = nc.dram_tensor("x2_scratch", (B, L, D), f32, kind="Internal").ap()
    x_t = x.rearrange("b (k p) c -> b p k c", p=128)
    v_t = ctx_v.rearrange("b (k p) c -> b p k c", p=128)
    x2_t = x2.rearrange("b (k p) c -> b p k c", p=128)
    x_rows = x.rearrange("b (k p) c -> (b k) p c", p=128)
    x2_rows = x2.rearrange("b (k p) c -> (b k) p c", p=128)
    out_rows = out.rearrange("b (k p) c -> (b k) p c", p=128)

    whole = ExitStack()
    with whole:
        def sem(name):
            return whole.enter_context(nc.semaphore(name))

        def keep(name, shape, dt=f32):
            return whole.enter_context(nc.sbuf_tensor(name, shape, dt))

        ident = keep("ident", [128, 128])
        gates_raw = keep("gates_raw", [128, 2])
        gates = keep("gates", [128, 2])
        norm = keep("norm", [128, D])
        bank = [whole.enter_context(nc.psum_tensor(f"bank{n}", [128, 512], f32)) for n in range(8)]

        b_loaded = sem("b_loaded")
        ident_loaded, gates_loaded, gates_ready = sem("ident_loaded"), sem("gates_loaded"), sem("gates_ready")

        with ExitStack() as s:
            def sb(name, shape, dt=f32):
                return s.enter_context(nc.sbuf_tensor(name, shape, dt))

            def both(t):
                return t[:, :].bitcast(f16).rearrange("p (h a c) -> p h a c", h=2, a=4)

            def four(t):
                return t[:, :].rearrange("p (a c) -> p a c", a=4)

            table = sb("table", [128, INV])
            table16 = sb("table16", [128, 2 * (FWD + INV)], f16)
            inv = table[:, :].rearrange("p (a q) -> p a q", a=4)
            fwd16 = table16[:, 0:2 * FWD].rearrange("p (h a j g) -> p h a j g", h=2, a=6, j=2)
            inv16 = table16[:, 2 * FWD:2 * (FWD + INV)].rearrange("p (h a q) -> p h a q", h=2, a=4)
            xt_mem = sb("xt", [128, TT * C])
            xt, q16 = four(xt_mem), both(xt_mem)
            qf = sb("qf", [128, TT, C])
            vt_mem = sb("vt", [128, TT * C])
            vt, k16 = four(vt_mem), both(vt_mem)
            v_last = sb("v_last", [128, C])
            kf = sb("kf", [128, TT, C])
            v16 = sb("v16", [128, 2, 2, C], f16)
            spec_v1 = sb("spec_v1", [128, 2, 4, C])
            spec_v = sb("spec_v", [128, 2, 4, C])
            prod_a = sb("prod_a", [128, 4, C])
            prod_b_mem = sb("prod_b", [128, 4 * C])
            prod_b, p16 = four(prod_b_mem), both(prod_b_mem)
            halves = sb("halves", [128, CT, C])
            corr = sb("corr", [128, CT, C])
            top = sb("top", [128, CT, 16])
            neg_max, w_sum, w_inv = sb("neg_max", [128, CT]), sb("w_sum", [128, CT]), sb("w_inv", [128, CT])
            w16 = sb("w16", [128, 2, TT, C], f16)
            spec_w = sb("spec_w", [128, 2, 5, C])
            spec_o = sb("spec_o", [128, 2, 4, C])
            term = sb("term", [128, 4, 2, C])
            eiz_scale = sb("eiz_scale", [128, 1])
            xres = sb("xres", [128, TT, C])
            xstat = sb("xstat", [128, TT, C])
            x_stats = sb("x_stats", [128, TT, NCH, 6])
            mv, var, std, tmp = sb("mv", [128, TT, 2]), sb("var", [128, TT]), sb("std", [128, TT]), sb("tmp", [128, TT])
            ln1_scale, ln1_bias = sb("ln1_scale", [128, TT]), sb("ln1_bias", [128, TT])
            v_dc = sb("v_dc", [1, C])
            dc_factor = sb("dc_factor", [1, 128])

            early = [prod_a[:, :, :], halves[:, :, :], corr[:, :, :], xres[:, :, :]]
            front, back = bank[0:3], bank[3:7]

            table16_loaded, table_loaded, dc_factor_set = sem("table16_loaded"), sem("table_loaded"), sem("dc_factor_set")
            x_loaded, v_loaded, v_last_loaded = sem("x_loaded"), sem("v_loaded"), sem("v_last_loaded")
            v_hi_made, v_lo_made, q_hi_made, q_lo_made = sem("v_hi_made"), sem("v_lo_made"), sem("q_hi_made"), sem("q_lo_made")
            p_hi_made, p_lo_made, w_lo_made = sem("p_hi_made"), sem("p_lo_made"), sem("w_lo_made")
            res_loaded, dc_loaded, x2_stored = sem("res_loaded"), sem("dc_loaded"), sem("x2_stored")
            early_loaded = [sem(f"early_loaded{n}") for n in range(NCH)]
            xstat_loaded, xstat_used = sem("xstat_loaded"), sem("xstat_used")
            ln1_var, ln1_sqrt, ln1_ready = sem("ln1_var"), sem("ln1_sqrt"), sem("ln1_ready")
            mv_made, ln1_step = sem("mv_made"), sem("ln1_step")
            x_normed, q_folded, v_shifted, k_folded = sem("x_normed"), sem("q_folded"), sem("v_shifted"), sem("k_folded")
            q_made, q_used, v_made, v_copied = sem("q_made"), sem("q_used"), sem("v_made"), sem("v_copied")
            prod_made, corr_made, halves_copied = sem("prod_made"), sem("corr_made"), sem("halves_copied")
            corr_ready, top_ready, exp_made, w_made, w_scaled = (sem("corr_ready"), sem("top_ready"), sem("exp_made"),
                                                                 sem("w_made"), sem("w_scaled"))
            w_turned, w_copied, wspec_made, wspec_copied = (sem("w_turned"), sem("w_copied"), sem("wspec_made"),
                                                            sem("wspec_copied"))
            term_made, term_added, dc_added, out_made, out_used = (sem("term_made"), sem("term_added"), sem("dc_added"),
                                                                   sem("out_made"), sem("out_used"))
            block = s.enter_context(nc.Block())

            LOOP, TURN = (2, STEPS - 6), NCH

            def least(i):
                return i if isinstance(i, int) else LOOP[0]

            def most(i):
                return i if isinstance(i, int) else LOOP[1] - 1

            def steps(eng, step):
                for i in range(LOOP[0]):
                    step(i, i % 2, i % NCH)
                with eng.Fori(0, (LOOP[1] - LOOP[0]) // TURN) as m:
                    for u in range(LOOP[0], LOOP[0] + TURN):
                        step(TURN * m + u, u % 2, u % NCH)
                for i in range(LOOP[1], STEPS + 1):
                    step(i, i % 2, i % NCH)

            OUT_ORDER = [2, 3, 0, 1]
            W_TABLES = [ER, EI, OR, OI]
            V_TABLES = [ER, OR, EI, OI]
            Q_TABLES = [ER, EIZ, ERZM, OR, OI]

            @block.sync
            def _(sp):
                def load_v(i):
                    if least(i) >= 1:
                        sp.wait_ge(v_made, 8 * i)
                    b, c = i // NCH, (i % NCH) * C
                    sp.nop(nofuse=True)
                    sp.dma_start(vt, v_t[b, :, :, ds(c, C)]).then_inc(v_loaded, 16)
                    sp.dma_start(v_last[:, :], ctx_v[b, L - 1:L, ds(c, C)].to_broadcast([128, C]))\
                      .then_inc(v_last_loaded, 16)

                def load_x(i):
                    if least(i) >= 1:
                        sp.wait_ge(q_made, 5 * i)
                    b, c = i // NCH, (i % NCH) * C
                    sp.nop(nofuse=True)
                    sp.dma_start(xt, x_t[b, :, :, ds(c, C)]).then_inc(x_loaded, 16)

                def load_res(i):
                    if least(i) >= 1:
                        sp.wait_ge(x2_stored, 16 * i)
                    b, c = i // NCH, (i % NCH) * C
                    sp.nop(nofuse=True)
                    sp.dma_start(xres[:, :, :], x_t[b, :, :, ds(c, C)]).then_inc(res_loaded, 16)
                    sp.dma_start(v_dc[:, :], ctx_v[b, L - 1:L, ds(c, C)]).then_inc(dc_loaded, 16)

                def store(i):
                    sp.wait_ge(out_used, 4 * (i + 1))
                    b, c = i // NCH, (i % NCH) * C
                    sp.nop(nofuse=True)
                    sp.dma_start(x2_t[b, :, :, ds(c, C)], xres[:, :, :]).then_inc(x2_stored, 16)

                def load_stats(n):
                    if least(n) > NCH:
                        sp.wait_ge(xstat_used, n)
                    sp.nop(nofuse=True)
                    b, c = n // NCH, (n % NCH) * C
                    sp.dma_start(xstat[:, :, :], x_t[b, :, :, ds(c, C)]).then_inc(xstat_loaded, 16)

                load_v(0)
                sp.dma_start(table16[:, :], tables16).then_inc(table16_loaded, 16)
                for n in range(NCH):
                    sp.dma_start(early[n], x_t[0, :, :, n * C:(n + 1) * C]).then_inc(early_loaded[n], 16)
                load_x(0)
                sp.dma_start(table[:, :], tables[:, 0:INV]).then_inc(table_loaded, 16)
                sp.dma_start(ident[:, :], tables[:, INV:INV + 128]).then_inc(ident_loaded, 16)
                sp.dma_start(gates_raw[:, 0:1], g_xattn.to_broadcast([128, 1])).then_inc(gates_loaded, 16)
                sp.dma_start(gates_raw[:, 1:2], g_ffn.to_broadcast([128, 1])).then_inc(gates_loaded, 16)
                load_stats(NCH)
                load_v(1)
                b_view = norm[:, :].rearrange("p (n e r) -> p n e r", e=E, r=R)
                for e in range(E):
                    sp.dma_start(b_view[:, :, e, :], b_w[e].rearrange("(n p) r -> p n r", p=128)).then_inc(b_loaded, 16)

                def step(i, par, phase):
                    if most(i) + NCH + 1 < STEPS:
                        load_stats(i + NCH + 1)
                    if most(i) + 1 < STEPS:
                        load_x(i + 1)
                    if least(i) >= 1:
                        load_res(i - 1)
                    if most(i) + 2 < STEPS:
                        load_v(i + 2)
                    if least(i) >= 1:
                        store(i - 1)

                steps(sp, step)
                sp.wait_ge(x2_stored, 16 * STEPS)

            @block.tensor
            def _(pe):
                def times3(to, weights, data, start, stop):
                    pe.matmul(to, weights[0], data[0], start=start, stop=False)
                    pe.matmul(to, weights[0], data[1], start=False, stop=False)
                    return pe.matmul(to, weights[1], data[0], start=False, stop=stop)

                def forward(to, tab, data):
                    for j in range(2):
                        mm = times3(to, [fwd16[:, h, tab, j, :] for h in range(2)], [data(h, j) for h in range(2)],
                                    j == 0, j == 1)
                    return mm

                def v_spectra(i):
                    for n in range(8):
                        if n < 4:
                            if least(i) >= 1:
                                pe.wait_ge(halves_copied, 4 * (i - 1) + n + 1)
                            if n == 0:
                                pe.wait_ge(v_lo_made, 3 * (i + 1))
                        else:
                            pe.wait_ge(v_copied, 8 * i + n - 3)
                        tab = V_TABLES[n % 4]
                        fold = 2 if tab >= OR else 0
                        forward(back[n % 4][:, :], tab,
                                (lambda h, j: k16[:, h, fold + j, :]) if n < 4 else (lambda h, j: v16[:, h, j, :]))\
                            .then_inc(v_made, 1)

                def q_spectra(i, first, last):
                    for n in range(first, last):
                        if n >= 3:
                            pe.wait_ge(q_used, 5 * i + n - 2)
                        elif least(i) >= 2:
                            pe.wait_ge(wspec_copied, 8 * (i - 1))
                        elif i == 1:
                            pe.wait_ge(q_used, 5)
                        if n == 0:
                            pe.wait_ge(q_lo_made, 2 * i + 1)
                        if n == 3:
                            pe.wait_ge(q_lo_made, 2 * i + 2)
                        tab = Q_TABLES[n]
                        fold = 2 if tab >= OR else 0
                        forward(front[n % 3][:, :], tab, lambda h, j: q16[:, h, fold + j, :]).then_inc(q_made, 1)

                def turn_w(c):
                    for j in range(TT):
                        if least(c) >= 1:
                            pe.wait_ge(out_used, 4 * (c - 1) + j + 1)
                        else:
                            pe.wait_ge(v_copied, 8 + 4 + j + 1)
                        for ct in range(CT):
                            if j == 0:
                                pe.wait_ge(w_scaled, 4 * c + ct + 1)
                            mm = pe.transpose(back[j][:, ct * 128:(ct + 1) * 128], corr[:, ct, j * 128:(j + 1) * 128],
                                              ident[:, :])
                        mm.then_inc(w_turned, 1)

                def w_spectra(c):
                    for k in range(8):
                        y, tab = k // 4, W_TABLES[k % 4]
                        if k >= 3:
                            pe.wait_ge(wspec_copied, 8 * c + k - 2)
                        elif most(c) + 1 < STEPS:
                            pe.wait_ge(q_used, 5 * (c + 1) + k + 3)
                        else:
                            pe.wait_ge(wspec_copied, 8 * c)
                        if k % 4 == 0:
                            pe.wait_ge(w_lo_made, 4 * c + 2 * y + 2)
                        forward(front[(5 + k) % 3][:, :], tab, lambda h, j: w16[:, h, 2 * y + j, :]).then_inc(wspec_made, 1)

                def correlate(i):
                    pe.wait_ge(p_lo_made, 2 * (i + 1))
                    for ct in range(CT):
                        if least(i) >= 1:
                            pe.wait_ge(w_lo_made, 4 * (i - 1) + ct + 1)
                        else:
                            pe.wait_ge(v_copied, 4 + ct + 1)
                        for o in range(2):
                            for k in range(2):
                                slot = o + 2 * k
                                mm = times3(back[ct][:, o * HALF:(o + 1) * HALF],
                                            [p16[:, h, slot, ct * 128:(ct + 1) * 128] for h in range(2)],
                                            [inv16[:, h, slot, :] for h in range(2)], k == 0, k == 1)
                        mm.then_inc(corr_made, 1)

                def out_tiles(c):
                    for j in range(TT):
                        if most(c) + 2 < STEPS:
                            pe.wait_ge(v_copied, 8 * (c + 2) + 4 + j + 1)
                        elif c + 2 == STEPS:
                            pe.wait_ge(halves_copied, 4 * (c + 1) + j + 1)
                        else:
                            pe.wait_ge(w_lo_made, 4 * c + j + 1)
                        if j == 0:
                            pe.wait_ge(dc_added, 3 * c + 2)
                        if j == 2:
                            pe.wait_ge(dc_added, 3 * c + 3)
                        h, p = OUT_ORDER[j] // 2, OUT_ORDER[j] % 2
                        for slot in range(4):
                            mm = pe.matmul(back[j][:, :], inv[:, slot, p * 128:(p + 1) * 128], spec_o[:, h, slot, :],
                                           start=(slot == 0), stop=(slot == 3))
                        mm.then_inc(out_made, 1)

                pe.wait_ge(table16_loaded, 16)
                v_spectra(0)
                pe.wait_ge(table_loaded, 16)
                pe.wait_ge(ident_loaded, 16)

                def step(i, par, phase):
                    if most(i) < STEPS:
                        q_spectra(i, 0, 3)
                    if least(i) >= 1:
                        turn_w(i - 1)
                    if most(i) < STEPS:
                        q_spectra(i, 3, 5)
                    if least(i) >= 1:
                        w_spectra(i - 1)
                    if most(i) < STEPS:
                        correlate(i)
                    if most(i) + 1 < STEPS:
                        v_spectra(i + 1)
                    if least(i) >= 1:
                        out_tiles(i - 1)

                steps(pe, step)

            @block.scalar
            def _(act):
                def normalise(i):
                    act.wait_ge(x_loaded, 16 * (i + 1))
                    act.wait_ge(ln1_ready, i // NCH + 1)
                    for t in range(TT):
                        act.activation(xt[:, t, :], xt[:, t, :], ACT.Identity, bias=ln1_bias[:, t:t + 1],
                                       scale=ln1_scale[:, t:t + 1]).then_inc(x_normed, 1)

                def copy_v(i, par, first=0, last=8):
                    for n in range(first, last):
                        if n % 4 == 0 and least(i) >= 2:
                            act.wait_ge(term_made, 12 * (i - 2) + (4 if n == 0 else 12))
                        act.wait_ge(v_made, 8 * i + n + 1)
                        to = (spec_v if n < 4 else spec_v1)[:, par, n % 4, :]
                        act.activation(to, back[n % 4][:, :], ACT.Copy, scale=V_SCALE / T_SCALE).then_inc(v_copied, 1)

                def high_v(i):
                    act.wait_ge(v_shifted, 4 * i + 2)
                    act.activation(v16[:, 0, :, :], vt[:, 2:4, :], ACT.Copy).then_inc(v_hi_made, 1)
                    act.wait_ge(k_folded, 4 * (i + 1))
                    for f in (0, 2):
                        act.activation(k16[:, 0, f:f + 2, :], kf[:, f:f + 2, :], ACT.Copy).then_inc(v_hi_made, 1)

                def high_q(i):
                    act.wait_ge(q_folded, 4 * (i + 1))
                    for f in (0, 2):
                        act.activation(q16[:, 0, f:f + 2, :], qf[:, f:f + 2, :], ACT.Copy).then_inc(q_hi_made, 1)

                def high_p(i):
                    act.wait_ge(prod_made, 2 * (i + 1))
                    for f in (0, 2):
                        act.activation(p16[:, 0, f:f + 2, :], prod_a[:, f:f + 2, :], ACT.Copy).then_inc(p_hi_made, 1)

                def copy_w(c):
                    if least(c) >= 1:
                        act.wait_ge(wspec_made, 8 * c)
                    for j in range(TT):
                        act.wait_ge(w_turned, 4 * c + j + 1)
                        act.activation(w16[:, 0, j, :], back[j][:, :], ACT.Copy).then_inc(w_copied, 1)

                def copy_wspec(c, first, last):
                    if first == 0 and least(c) >= 1:
                        act.wait_ge(term_made, 12 * c)
                    for k in range(first, last):
                        y, tab, view = k // 4, W_TABLES[k % 4], front[(5 + k) % 3]
                        act.wait_ge(wspec_made, 8 * c + k + 1)
                        if tab == EI:
                            act.wait_ge(wspec_copied, 8 * c + k)
                            act.activation(spec_w[0:1, y, 1, :], view[0:1, :], ACT.Copy, scale=1.0 / (V_SCALE * T_SCALE))
                            op = act.activation(spec_w[:, y, 3, :], view[:, :], ACT.Copy, scale=eiz_scale[:, :])
                        else:
                            for slot in {ER: (1, 0), OR: (2,), OI: (4,)}[tab]:
                                op = act.activation(spec_w[:, y, slot, :], view[:, :], ACT.Copy,
                                                    scale=1.0 / (V_SCALE * T_SCALE))
                        op.then_inc(wspec_copied, 1)

                def copy_halves(i):
                    if least(i) >= 1:
                        act.wait_ge(w_made, 4 * i)
                    for ct in range(CT):
                        act.wait_ge(corr_made, 4 * i + ct + 1)
                        act.activation(halves[:, ct, :], back[ct][:, :], ACT.Copy, scale=1.0 / T_SCALE).then_inc(halves_copied, 1)

                def exponentials(i):
                    act.wait_ge(top_ready, 1 + 4 * i)
                    for ct in range(CT):
                        act.activation(halves[:, ct, :], corr[:, ct, :], ACT.Exp, bias=neg_max[:, ct:ct + 1])\
                           .then_inc(exp_made, 1)

                def scale_w(i):
                    act.wait_ge(top_ready, 4 * (i + 1))
                    for ct in range(CT):
                        act.activation(corr[:, ct, :], corr[:, ct, :], ACT.Copy, scale=w_inv[:, ct:ct + 1])\
                           .then_inc(w_scaled, 1)

                def deviation(b):
                    act.wait_ge(ln1_var, b + 1)
                    act.activation(std[:, :], var[:, :], ACT.Sqrt).then_inc(ln1_sqrt, 1)

                high_v(0)
                deviation(0)
                copy_v(0, 0, 0, 4)
                normalise(0)
                copy_v(0, 0, 4, 8)
                high_q(0)
                act.wait_ge(dc_factor_set, 3)
                act.wait_ge(gates_loaded, 32)
                act.activation(gates[:, :], gates_raw[:, :], ACT.Tanh).then_inc(gates_ready, 1)

                def step(i, par, phase):
                    if least(i) >= 1:
                        copy_w(i - 1)
                    if most(i) + 1 < STEPS:
                        high_v(i + 1)
                    if least(i) >= 1:
                        copy_wspec(i - 1, 0, 4)
                    if most(i) < STEPS:
                        high_p(i)
                    if least(i) >= 1:
                        copy_wspec(i - 1, 4, 8)
                    if most(i) + 1 < STEPS:
                        normalise(i + 1)
                    if phase == NCH - 2 and most(i) + NCH < STEPS:
                        deviation(i // NCH + 1)
                    if most(i) < STEPS:
                        copy_halves(i)
                    if most(i) == 0:
                        high_q(1)
                    if most(i) + 1 < STEPS:
                        copy_v(i + 1, 1 - par)
                    if most(i) < STEPS:
                        exponentials(i)
                    if least(i) >= 1 and most(i) + 1 < STEPS:
                        high_q(i + 1)
                    if most(i) < STEPS:
                        scale_w(i)

                steps(act, step)

            @block.vector
            def _(dve):
                def q_times_k(i, par, first, last):
                    if first == 0:
                        dve.wait_ge(v_copied, 8 * i + 4)
                        if least(i) >= 1:
                            dve.wait_ge(corr_made, 4 * i)
                    k = spec_v[:, par]
                    uses = [[(prod_a, 0, 0)], [(prod_b, 0, 2), (prod_a, 2, 0)], [(prod_b, 2, 2)],
                            [(prod_a, 1, 1), (prod_b, 3, 3)], [(prod_b, 1, 3), (prod_a, 3, 1)]]
                    for n in range(first, last):
                        dve.wait_ge(q_made, 5 * i + n + 1)
                        for to, slot, kslot in uses[n]:
                            op = dve.tensor_tensor(to[:, slot, :], front[n % 3][:, :], k[:, kslot, :], ALU.mult)
                        op.then_inc(q_used, 1)

                def low_w(c):
                    if least(c) >= 1:
                        dve.wait_ge(wspec_made, 8 * c)
                    for j in range(TT):
                        dve.wait_ge(w_copied, 4 * c + j + 1)
                        dve.tensor_tensor(w16[:, 1, j, :], back[j][:, :], w16[:, 0, j, :], ALU.subtract)\
                           .then_inc(w_lo_made, 1)

                def low_v(i):
                    dve.wait_ge(v_lo_made, 3 * i + 1)
                    for n, f in enumerate((0, 2)):
                        dve.wait_ge(v_hi_made, 3 * i + n + 2)
                        dve.tensor_tensor(k16[:, 1, f:f + 2, :], kf[:, f:f + 2, :], k16[:, 0, f:f + 2, :], ALU.subtract)\
                           .then_inc(v_lo_made, 1)

                def low_q(i):
                    for n, f in enumerate((0, 2)):
                        dve.wait_ge(q_hi_made, 2 * i + n + 1)
                        dve.tensor_tensor(q16[:, 1, f:f + 2, :], qf[:, f:f + 2, :], q16[:, 0, f:f + 2, :], ALU.subtract)\
                           .then_inc(q_lo_made, 1)

                def low_p(i):
                    for n, f in enumerate((0, 2)):
                        dve.wait_ge(p_hi_made, 2 * i + n + 1)
                        dve.tensor_tensor(p16[:, 1, f:f + 2, :], prod_a[:, f:f + 2, :], p16[:, 0, f:f + 2, :], ALU.subtract)\
                           .then_inc(p_lo_made, 1)

                def v_times_w(c, par, first, last):
                    v1r, v1i = spec_v1[:, par, 0:2, :], spec_v1[:, par, 2:4, :]
                    vr, vi = spec_v[:, par, 0:2, :], spec_v[:, par, 2:4, :]
                    r, rz, im = ([spec_w[:, y, 0:3:2, :] for y in range(2)], [spec_w[:, y, 1:3, :] for y in range(2)],
                                 [spec_w[:, y, 3:5, :] for y in range(2)])
                    o1r, o1i, o0r, o0i = spec_o[:, 1, 0:2, :], spec_o[:, 1, 2:4, :], spec_o[:, 0, 0:2, :], spec_o[:, 0, 2:4, :]
                    todo = [(o0r, vr, r[0]), (None, vi, im[0]), (o0i, vi, rz[0]), (None, vr, im[0]),
                            (o1r, v1r, r[0]), (None, v1i, im[0]), (o1i, v1i, rz[0]), (None, v1r, im[0]),
                            (None, v1r, r[1]), (None, v1i, rz[1]), (None, v1i, im[1]), (None, v1r, im[1])]
                    if first == 0:
                        if least(c) >= 1:
                            dve.wait_ge(out_made, 4 * c)
                            dve.wait_ge(term_added, 8 * c)
                        dve.wait_ge(wspec_copied, 8 * c + 4)
                    t = sum(to is None for to, _, _ in todo[:first])
                    for n, (to, a, w) in list(enumerate(todo))[first:last]:
                        if n == 8:
                            dve.wait_ge(wspec_copied, 8 * c + 8)
                        if to is None:
                            if t >= 4:
                                dve.wait_ge(term_added, 8 * c + t - 3)
                            to = term[:, t % 4]
                            t += 1
                        dve.tensor_tensor(to, a, w, ALU.mult).then_inc(term_made, 1)

                def largest(i):
                    if least(i) >= 1:
                        dve.wait_ge(w_turned, 4 * i)
                    dve.wait_ge(p_lo_made, 2 * (i + 1))
                    dve.wait_ge(halves_copied, 4 * (i + 1))
                    e, o = halves[:, :, 0:HALF], halves[:, :, HALF:C]
                    dve.tensor_tensor(corr[:, :, 0:HALF], e, o, ALU.add).then_inc(corr_ready, 4)
                    dve.tensor_tensor(corr[:, :, HALF:C], e, o, ALU.subtract).then_inc(corr_ready, 4)
                    base = 20 * i
                    dve.wait_ge(corr_ready, base + 8)
                    for ct in range(CT):
                        if ct == 0:
                            dve.nop(nofuse=True)
                        dve.max(top[:, ct, 0:8], corr[:, ct, :]).then_inc(corr_ready, 1)
                    dve.wait_ge(corr_ready, base + 12)
                    dve.tensor_scalar(neg_max[:, :], top[:, :, 0], -1.0, None, ALU.mult).then_inc(top_ready, 1)
                    for ct in range(CT):
                        dve.match_replace(prod_a[:, ct, :], top[:, ct, 0:8], corr[:, ct, :], -3.0e38)\
                           .then_inc(corr_ready, 1)
                    for ct in range(CT):
                        dve.wait_ge(corr_ready, base + 12 + ct + 1)
                        dve.nop(nofuse=True)
                        dve.max(top[:, ct, 8:16], prod_a[:, ct, :]).then_inc(corr_ready, 1)
                def select(i):
                    for ct in range(CT):
                        dve.wait_ge(corr_ready, 20 * i + 16 + ct + 1)
                        dve.wait_ge(exp_made, 4 * i + ct + 1)
                        dve.scalar_tensor_tensor(out=corr[:, ct, :], in0=corr[:, ct, :], scalar=top[:, ct, TOPK - 1:TOPK],
                                                 in1=halves[:, ct, :], op0=ALU.is_ge, op1=ALU.mult,
                                                 accum_out=w_sum[:, ct:ct + 1]).then_inc(w_made, 1)
                    dve.wait_ge(w_made, 4 * (i + 1))
                    dve.reciprocal(w_inv[:, :], w_sum[:, :]).then_inc(top_ready, 3)

                def residual(c):
                    dve.wait_ge(res_loaded, 16 * (c + 1))
                    for j in range(TT):
                        t = OUT_ORDER[j]
                        dve.wait_ge(out_made, 4 * c + j + 1)
                        dve.scalar_tensor_tensor(out=xres[:, t, :], in0=back[j][:, :], scalar=gates[:, 0:1],
                                                 in1=xres[:, t, :], op0=ALU.mult, op1=ALU.add).then_inc(out_used, 1)

                def take_stats(n, chunk, early_from=None):
                    if early_from is not None:
                        dve.wait_ge(early_loaded[chunk], 16)
                    else:
                        dve.wait_ge(xstat_loaded, 16 * (n - NCH + 1))
                    x_from = xstat[:, :, :] if early_from is None else early_from
                    for t in range(TT):
                        op = dve.bn_stats(x_stats[:, t, chunk, :], x_from[:, t, :])
                    op.then_inc(xstat_used, 1)

                def variance(b):
                    dve.wait_ge(xstat_used, NCH * (b + 1))
                    dve.nop(nofuse=True)
                    for t in range(TT):
                        op = dve.bn_aggr(mv[:, t, :], x_stats[:, t, :, :].rearrange("p a b -> p (a b)"))
                    op.then_inc(mv_made, 1)
                    dve.wait_ge(mv_made, b + 1)
                    dve.tensor_scalar(var[:, :], mv[:, :, 1], EPS, None, ALU.add).then_inc(ln1_var, 1)

                def scales(b):
                    newton(dve, ln1_step, 6 * b, ln1_sqrt, b + 1, var, std, tmp, mv[:, :, 0], ln1_scale, ln1_bias, 1.0)
                    dve.wait_ge(ln1_step, 6 * (b + 1))
                    dve.tensor_copy(tmp[:, :], ln1_bias[:, :]).then_inc(ln1_ready, 1)

                def step(i, par, phase):
                    if most(i) < STEPS:
                        q_times_k(i, par, 0, 3)
                    if least(i) >= 1:
                        low_w(i - 1)
                    if most(i) < STEPS:
                        q_times_k(i, par, 3, 5)
                    more = most(i) + NCH + 1 < STEPS
                    if most(i) + 1 < STEPS:
                        low_v(i + 1)
                    if more:
                        take_stats(i + NCH + 1, (phase + 1) % NCH)
                    if more and phase == NCH - 2:
                        variance(i // NCH + 1)
                    if least(i) >= 1:
                        v_times_w(i - 1, 1 - par, 0, 2)
                    if most(i) < STEPS:
                        low_p(i)
                    if least(i) >= 1:
                        v_times_w(i - 1, 1 - par, 2, 12)
                    if most(i) == 0:
                        low_q(1)
                    if most(i) < STEPS:
                        largest(i)
                        select(i)
                    if least(i) >= 1 and most(i) + 1 < STEPS:
                        low_q(i + 1)
                    if least(i) >= 1:
                        residual(i - 1)
                    if more and phase == NCH - 2:
                        dve.wait_ge(x_normed, 4 * (i + 2))
                        scales(i // NCH + 1)

                for n in range(NCH):
                    if n == 2:
                        low_v(0)
                    take_stats(n, n, early[n])
                variance(0)
                scales(0)
                low_q(0)
                dve.wait_ge(gates_ready, 1)
                take_stats(NCH, 0)
                steps(dve, step)

            @block.gpsimd
            def _(pool):
                def prepare_v(i):
                    pool.wait_ge(v_loaded, 16 * (i + 1))
                    pool.wait_ge(v_last_loaded, 16 * (i + 1))
                    if least(i) >= 1:
                        pool.wait_ge(v_lo_made, 3 * i)
                    for t in (2, 3, 0, 1):
                        pool.tensor_tensor(vt[:, t, :], vt[:, t, :], v_last[:, :], ALU.subtract)\
                            .then_inc(v_shifted, 1)
                    pool.wait_ge(v_shifted, 4 * (i + 1))
                    for j in range(4):
                        pool.tensor_tensor(kf[:, j, :], vt[:, j % 2, :], vt[:, 2 + j % 2, :],
                                           ALU.add if j < 2 else ALU.subtract).then_inc(k_folded, 1)

                def low_v1(i):
                    pool.wait_ge(v_hi_made, 3 * i + 1)
                    pool.tensor_tensor(v16[:, 1, :, :], vt[:, 2:4, :], v16[:, 0, :, :], ALU.subtract).then_inc(v_lo_made, 1)

                def fold_q(i):
                    if least(i) >= 1:
                        pool.wait_ge(q_lo_made, 2 * i)
                    pool.wait_ge(x_normed, 4 * (i + 1))
                    for j in range(4):
                        pool.tensor_tensor(qf[:, j, :], xt[:, j % 2, :], xt[:, 2 + j % 2, :],
                                           ALU.add if j < 2 else ALU.subtract).then_inc(q_folded, 1)

                def sum_qk(i):
                    pool.wait_ge(q_used, 5 * (i + 1))
                    pool.tensor_tensor(prod_a[:, 0:2, :], prod_a[:, 0:2, :], prod_b[:, 0:2, :], ALU.add)\
                        .then_inc(prod_made, 1)
                    pool.tensor_tensor(prod_a[:, 2:4, :], prod_a[:, 2:4, :], prod_b[:, 2:4, :], ALU.subtract)\
                        .then_inc(prod_made, 1)

                def sum_vw(c):
                    o1r, o1i, o0r, o0i = spec_o[:, 1, 0:2, :], spec_o[:, 1, 2:4, :], spec_o[:, 0, 0:2, :], spec_o[:, 0, 2:4, :]
                    todo = [(o0r, ALU.add, 2, 0), (o0i, ALU.subtract, 4, 0), (o1r, ALU.add, 6, 0),
                            (o1i, ALU.subtract, 8, 0), (o0r, ALU.add, 9, 1), (o0i, ALU.add, 10, 2),
                            (o0r, ALU.add, 11, 5), (o0i, ALU.subtract, 12, 6)]
                    pool.wait_ge(dc_loaded, 16 * (c + 1))
                    dc_row = v_dc[:, :].rearrange("p (a c) -> p a c", c=128)
                    pool.tensor_tensor(dc_row, dc_row, dc_factor[:, :].rearrange("p (a c) -> p a c", a=1).to_broadcast([1, CT, 128]),
                                       ALU.mult).then_inc(dc_added, 1)
                    dc_at = {3: 1, 7: 0}
                    for t, (to, sign, made, own) in enumerate(todo):
                        pool.wait_ge(term_made, 12 * c + made)
                        if own:
                            pool.wait_ge(term_added, 8 * c + own)
                        pool.tensor_tensor(to, to, term[:, t % 4], sign).then_inc(term_added, 1)
                        if t in dc_at:
                            if t == 3:
                                pool.wait_ge(dc_added, 3 * c + 1)
                            pool.wait_ge(term_added, 8 * c + t + 1)
                            dc = spec_o[0:1, dc_at[t], 0, :]
                            pool.tensor_tensor(dc, dc, v_dc[:, :], ALU.add).then_inc(dc_added, 1)

                pool.memset(dc_factor[:, :], float(L)).then_inc(dc_factor_set, 1)
                pool.memset(eiz_scale[:, :], 1.0 / (V_SCALE * T_SCALE)).then_inc(dc_factor_set, 1)
                pool.wait_ge(dc_factor_set, 2)
                pool.memset(eiz_scale[0:1, :], 0.0).then_inc(dc_factor_set, 1)
                prepare_v(0)
                low_v1(0)
                fold_q(0)

                def step(i, par, phase):
                    if most(i) + 1 < STEPS:
                        prepare_v(i + 1)
                        low_v1(i + 1)
                    if most(i) < STEPS:
                        sum_qk(i)
                    if least(i) >= 1:
                        sum_vw(i - 1)
                    if most(i) + 1 < STEPS:
                        fold_q(i + 1)

                steps(pool, step)

        with ExitStack() as s:
            def sb(name, shape, dt=f32):
                return s.enter_context(nc.sbuf_tensor(name, shape, dt))

            w_hi, w_lo = sb("w_hi", [128, KD, D], f16), sb("w_lo", [128, KD, D], f16)
            ag_hi, ag_lo = sb("ag_hi", [128, KD, NG], f16), sb("ag_lo", [128, KD, NG], f16)
            b_hi, b_lo = sb("b_hi", [128, D], f16), sb("b_lo", [128, D], f16)
            row = sb("row", [128, 2, D])
            wrow = sb("wrow", [128, 2, D])
            nt_hi, nt_lo = sb("nt_hi", [128, KD, 128], f16), sb("nt_lo", [128, KD, 128], f16)
            bias = sb("bias", [128, D])
            ln2_scale, ln2_bias = sb("ln2_scale", [128, 1]), sb("ln2_bias", [128, 1])
            stats, mv = sb("stats2", [128, NCH, 6]), sb("mv2", [128, 2])
            var, std, tmp = sb("var2", [128, 1]), sb("std2", [128, 1]), sb("tmp2", [128, 1])
            thr_b, out_gate = sb("thr_b", [128, 1]), sb("out_gate", [128, 1])
            logit = sb("logit", [128, NG])
            lmax, esum, erec, wsum, wzero = (sb(n, [128, 1]) for n in ("lmax", "esum", "erec", "wsum", "wzero"))
            thr = sb("thr", [128, 1])
            gate = sb("gate", [128, E])
            hw = sb("hw", [128, E * R])
            hwt_hi, hwt_lo = sb("hwt_hi", [128, 128], f16), sb("hwt_lo", [128, 128], f16)

            row_loaded = [sem(f"row_loaded{n}") for n in range(4)]
            small_loaded = sem("small_loaded")
            wt_made, wt_hi, wt_lo = sem("wt_made"), sem("wt_hi"), sem("wt_lo")
            ln2_step, ln2_sqrt, bias_ready = sem("ln2_step"), sem("ln2_sqrt"), sem("bias_ready")

            NW = D // 128
            JOBS = NW + 3
            EARLY = 4
            DESCALE = 1.0 / (N_SCALE * W_SCALE)

            def weight_row(n):
                m = n - 1
                return (row if m % 4 < 2 else wrow)[:, m % 2, :]

            def weight_target(n, q, part):
                if n == 0:
                    return (b_hi, b_lo)[part][:, 512 * q:512 * (q + 1)].rearrange("p (k c) -> p k c", k=4)
                if n <= NW:
                    return (w_hi, w_lo)[part][:, 4 * q:4 * q + 4, (n - 1) * 128:n * 128]
                t = (ag_hi, ag_lo)[part]
                return t[:, 4 * q:4 * q + 4, 0:128] if n == NW + 1 else t[:, 4 * q:4 * q + 4, 128:NG]

            def weight_bank(n, q):
                cols = 128 if n <= NW + 1 else E + 1
                view = bank[(4 * n + q) % 8][:, 0:4 * cols] if cols == 128 else bank[(4 * n + q) % 8][:, 0:4 * 16]
                view = view.rearrange("p (k c) -> p k c", k=4)
                return view if cols == 128 else view[:, :, 0:cols]

            first_loaded = sem("first_loaded")
            x2_loaded = [sem("x2_loaded0"), sem("x2_loaded1")]
            out_stored = [sem("out_stored0"), sem("out_stored1")]
            normed, turned, nt_hi_made, nt_lo_made = sem("normed"), sem("turned"), sem("nt_hi_made"), sem("nt_lo_made")
            logits_made, logits_copied, exps_made, gate_step = (sem("logits_made"), sem("logits_copied"),
                                                                sem("exps_made"), sem("gate_step"))
            hw_turned, hwt_hi_made, hwt_lo_made = sem("hw_turned"), sem("hwt_hi_made"), sem("hwt_lo_made")
            base_made = sem("base_made")
            bias_added, dense_made, out_ready = sem("bias_added"), sem("dense_made"), sem("out_ready")
            dense, turn_bank, logit_bank, hw_bank = bank[0:4], bank[4:6], bank[6], bank[7]
            GATE_OPS, LN2_OPS = 11, 9

            FLOOP = (2, ROWS - 2)

            def fleast(i):
                return i if isinstance(i, int) else FLOOP[0]

            def fmost(i):
                return i if isinstance(i, int) else FLOOP[1] - 1

            def tiles(eng, step):
                for i in range(FLOOP[0]):
                    step(i, i % 2)
                with eng.Fori(0, (FLOOP[1] - FLOOP[0]) // 2) as m:
                    for u in range(2):
                        step(2 * m + (FLOOP[0] + u), u)
                for i in range(FLOOP[1], ROWS):
                    step(i, i % 2)

            with nc.Block() as block:
                @block.sync
                def _(sp):
                    def x2_first():
                        sp.wait_ge(wt_made, 4)
                        sp.dma_start(norm[:, :], x2_rows[0]).then_inc(first_loaded, 16)

                    for m in range(JOBS - 1):
                        n = m + 1
                        if m >= 4:
                            sp.wait_ge(wt_made, 4 * (n - 3))
                        to, loaded = weight_row(n), row_loaded[m % 4]
                        if n <= NW:
                            sp.dma_start(to, w_base[m * 128:(m + 1) * 128, :]).then_inc(loaded, 16)
                        elif n == NW + 1:
                            sp.dma_start(to, a_w.rearrange("e r d -> (e r) d")).then_inc(loaded, 16)
                        else:
                            sp.dma_start(to[0:E, :], w_gate).then_inc(loaded, 16)
                            sp.dma_start(to[E:E + 1, :], w_thr.rearrange("(a n) -> a n", a=1)).then_inc(loaded, 16)
                        if m == 2:
                            x2_first()
                    sp.dma_start(bias[:, :], b_base.rearrange("(a n) -> a n", a=1).to_broadcast([128, D])).then_inc(small_loaded, 16)
                    sp.dma_start(thr_b[:, :], b_thr.to_broadcast([128, 1])).then_inc(small_loaded, 16)

                    def load(i, par):
                        if fleast(i) >= 2:
                            sp.wait_ge(out_stored[par], 16 * (i // 2))
                        sp.nop(nofuse=True)
                        sp.dma_start(row[:, par, :], x2_rows[i]).then_inc(x2_loaded[par], 16)

                    def step(i, par):
                        if fmost(i) + 1 < ROWS:
                            load(i + 1, 1 - par)
                        sp.wait_ge(out_ready, 4 * (i + 1))
                        sp.nop(nofuse=True)
                        sp.dma_start(out_rows[i], row[:, par, :]).then_inc(out_stored[par], 16)

                    sp.wait_ge(wt_made, 4 * (JOBS - 1))
                    load(0, 0)
                    sp.wait_ge(wt_made, 4 * JOBS)
                    tiles(sp, step)
                    for par in range(2):
                        sp.wait_ge(out_stored[par], 16 * ROWS // 2)

                @block.tensor
                def _(pe):
                    for n in range(JOBS):
                        if n == 0:
                            pe.wait_ge(b_loaded, 16 * E)
                        else:
                            m = n - 1
                            pe.wait_ge(row_loaded[m % 4], 16 * (m // 4 + 1) + (16 if n == JOBS - 1 else 0))
                        rows, source = (128 if n <= NW + 1 else E + 1), (weight_row(n) if n else norm)
                        for q in range(4):
                            if 4 * n + q >= 8:
                                pe.wait_ge(wt_hi, 4 * n + q - 7)
                                pe.wait_ge(wt_lo, 4 * n + q - 7)
                            view = weight_bank(n, q)
                            for k in range(4):
                                d = (4 * q + k) * 128
                                mm = pe.transpose(view[:, k, :], source[0:rows, d:d + 128], ident[0:rows, 0:rows])
                            mm.then_inc(wt_made, 1)

                    def turn(i, first, last):
                        if first == 0:
                            pe.wait_ge(normed, i + 1)
                        for q in range(first, last):
                            if q >= 2 or fleast(i) >= 1:
                                pe.wait_ge(nt_hi_made, 4 * i + q - 1)
                                pe.wait_ge(nt_lo_made, 4 * i + q - 1)
                            for k in range(4):
                                d = (4 * q + k) * 128
                                mm = pe.transpose(turn_bank[q % 2][:, k * 128:(k + 1) * 128], norm[:, d:d + 128], ident[:, :])
                            mm.then_inc(turned, 1)

                    def logits(i):
                        if fleast(i) >= 1:
                            pe.wait_ge(logits_copied, i)
                        acc = logit_bank[:, 0:NG]
                        for k in range(KD):
                            if k % 4 == 0:
                                pe.wait_ge(nt_hi_made, 4 * i + k // 4 + 1)
                                pe.wait_ge(nt_lo_made, 4 * i + k // 4 + 1)
                            pe.matmul(acc, nt_hi[:, k, :], ag_hi[:, k, :], start=(k == 0), stop=False)
                            pe.matmul(acc, nt_hi[:, k, :], ag_lo[:, k, :], start=False, stop=False)
                            mm = pe.matmul(acc, nt_lo[:, k, :], ag_hi[:, k, :], start=False, stop=(k == KD - 1))
                        mm.then_inc(logits_made, 1)

                    def base(i):
                        for k in range(KD):
                            for n, (a, w) in enumerate(((nt_hi, w_hi), (nt_hi, w_lo), (nt_lo, w_hi))):
                                for o in range(4):
                                    if k == 0 and n == 0 and fleast(i) >= 1:
                                        pe.wait_ge(out_ready, 4 * (i - 1) + o + 1)
                                    mm = pe.matmul(dense[o][:, :], a[:, k, :], w[:, k, o * 512:(o + 1) * 512],
                                                   start=(k == 0 and n == 0), stop=False)
                        mm.then_inc(base_made, 1)

                    def turn_hw(i):
                        pe.wait_ge(gate_step, GATE_OPS * (i + 1))
                        if fleast(i) >= 1:
                            pe.wait_ge(hwt_lo_made, i)
                        pe.transpose(hw_bank[:, 0:128], hw[:, :], ident[:, :]).then_inc(hw_turned, 1)

                    def experts(i):
                        pe.wait_ge(hwt_hi_made, i + 1)
                        pe.wait_ge(hwt_lo_made, i + 1)
                        for o in range(4):
                            cols = slice(o * 512, (o + 1) * 512)
                            pe.matmul(dense[o][:, :], hwt_hi[:, :], b_hi[:, cols], start=False, stop=False)
                            pe.matmul(dense[o][:, :], hwt_hi[:, :], b_lo[:, cols], start=False, stop=False)
                            pe.matmul(dense[o][:, :], hwt_lo[:, :], b_hi[:, cols], start=False, stop=True)\
                              .then_inc(dense_made, 1)

                    def step(i, par):
                        logits(i)
                        base(i)
                        turn_hw(i)
                        if fmost(i) + 1 < ROWS:
                            turn(i + 1, 0, 2)
                        experts(i)
                        if fmost(i) + 1 < ROWS:
                            turn(i + 1, 2, 4)

                    pe.wait_ge(wt_hi, 4 * JOBS)
                    pe.wait_ge(wt_lo, 4 * JOBS)
                    turn(0, 0, 4)
                    tiles(pe, step)

                @block.scalar
                def _(act):
                    def weights_hi(first, last):
                        for g in range(first, last):
                            act.wait_ge(wt_made, g + 1)
                            act.activation(weight_target(g // 4, g % 4, 0), weight_bank(g // 4, g % 4), ACT.Copy,
                                           scale=W_SCALE).then_inc(wt_hi, 1)

                    def normalise(i, x2):
                        act.wait_ge(ln2_step, LN2_OPS * i + 3)
                        act.activation(std[:, :], var[:, :], ACT.Sqrt).then_inc(ln2_sqrt, 1)
                        act.wait_ge(ln2_step, LN2_OPS * (i + 1))
                        if fleast(i) >= 1:
                            act.wait_ge(turned, 4 * i)
                        act.activation(norm[:, :], x2[:, :], ACT.Identity, bias=ln2_bias[:, :],
                                       scale=ln2_scale[:, :]).then_inc(normed, 1)

                    def turned_hi(i):
                        if fleast(i) >= 1:
                            act.wait_ge(base_made, i)
                        for q in range(4):
                            act.wait_ge(turned, 4 * i + q + 1)
                            act.activation(nt_hi[:, 4 * q:4 * q + 4, :].rearrange("p k t -> p (k t)"),
                                           turn_bank[q % 2][:, :], ACT.Copy).then_inc(nt_hi_made, 1)

                    def gating(i):
                        act.wait_ge(logits_made, i + 1)
                        if fleast(i) >= 1:
                            act.wait_ge(gate_step, GATE_OPS * i)
                        act.activation(logit[:, :], logit_bank[:, 0:NG], ACT.Copy, scale=DESCALE)\
                           .then_inc(logits_copied, 1)
                        act.wait_ge(gate_step, GATE_OPS * i + 1)
                        act.wait_ge(logits_copied, i + 1)
                        act.activation(gate[:, :], logit[:, E * R:E * R + E], ACT.Exp, bias=lmax[:, :],
                                       accum_out=esum[:, :]).then_inc(exps_made, 1)
                        act.activation(thr[:, :], logit[:, E * R + E:NG], ACT.Exp, bias=thr_b[:, :], scale=-1.0)\
                           .then_inc(exps_made, 1)

                    def hw_hi(i):
                        if fleast(i) >= 1:
                            act.wait_ge(dense_made, 4 * i)
                        act.wait_ge(hw_turned, i + 1)
                        act.activation(hwt_hi[:, :], hw_bank[:, 0:128], ACT.Copy).then_inc(hwt_hi_made, 1)

                    def step(i, par):
                        gating(i)
                        if fmost(i) + 1 < ROWS:
                            normalise(i + 1, row[:, 1 - par, :])
                        hw_hi(i)
                        if fmost(i) + 1 < ROWS:
                            turned_hi(i + 1)

                    weights_hi(0, 4 * EARLY)
                    normalise(0, norm)
                    weights_hi(4 * EARLY, 4 * JOBS)
                    turned_hi(0)
                    tiles(act, step)

                @block.vector
                def _(dve):
                    def weights_lo(first, last):
                        for g in range(first, last):
                            dve.wait_ge(wt_hi, g + 1)
                            dve.scalar_tensor_tensor(out=weight_target(g // 4, g % 4, 1), in0=weight_bank(g // 4, g % 4),
                                                     scalar=W_SCALE, in1=weight_target(g // 4, g % 4, 0), op0=ALU.mult,
                                                     op1=ALU.subtract).then_inc(wt_lo, 1)

                    def statistics(i, x2):
                        for q in range(NCH):
                            op = dve.bn_stats(stats[:, q, :], x2[:, q * C:(q + 1) * C])
                        op.then_inc(ln2_step, 1)
                        dve.wait_ge(ln2_step, LN2_OPS * i + 1)
                        dve.nop(nofuse=True)
                        dve.bn_aggr(mv[:, :], stats[:, :, :].rearrange("p a b -> p (a b)")).then_inc(ln2_step, 1)
                        dve.wait_ge(ln2_step, LN2_OPS * i + 2)
                        dve.tensor_scalar(var[:, :], mv[:, 1:2], EPS, None, ALU.add).then_inc(ln2_step, 1)
                        if fleast(i) >= 1:
                            dve.wait_ge(normed, i)
                        newton(dve, ln2_step, LN2_OPS * i + 3, ln2_sqrt, i + 1, var, std, tmp, mv[:, 0:1],
                               ln2_scale, ln2_bias, N_SCALE)

                    def turned_lo(i, first, last):
                        if first == 0 and fleast(i) >= 1:
                            dve.wait_ge(base_made, i)
                        for q in range(first, last):
                            dve.wait_ge(nt_hi_made, 4 * i + q + 1)
                            dve.tensor_tensor(nt_lo[:, 4 * q:4 * q + 4, :].rearrange("p k t -> p (k t)"),
                                              turn_bank[q % 2][:, :],
                                              nt_hi[:, 4 * q:4 * q + 4, :].rearrange("p k t -> p (k t)"),
                                              ALU.subtract).then_inc(nt_lo_made, 1)

                    def gating(i):
                        done = [0]

                        def chain(op):
                            op.then_inc(gate_step, 1)
                            done[0] += 1
                            if done[0] < GATE_OPS:
                                dve.wait_ge(gate_step, GATE_OPS * i + done[0])

                        dve.wait_ge(logits_copied, i + 1)
                        chain(dve.tensor_reduce(lmax[:, :], logit[:, E * R:E * R + E], AX.X, ALU.max, negate=True))
                        dve.wait_ge(exps_made, 2 * (i + 1))
                        chain(dve.reciprocal(erec[:, :], esum[:, :]))
                        chain(dve.tensor_scalar(thr[:, :], thr[:, :], 1.0, 1.0 / MAX_THRESHOLD, ALU.add, ALU.mult))
                        chain(dve.reciprocal(thr[:, :], thr[:, :]))
                        chain(dve.tensor_scalar(gate[:, :], gate[:, :], erec[:, :], thr[:, :], ALU.mult, ALU.subtract))
                        chain(dve.tensor_scalar(gate[:, :], gate[:, :], 0.0, None, ALU.max, ALU.add, accum_out=wsum[:, :]))
                        chain(dve.tensor_scalar(wzero[:, :], wsum[:, :], 0.0, None, ALU.is_equal))
                        chain(dve.tensor_tensor(wsum[:, :], wsum[:, :], wzero[:, :], ALU.add))
                        chain(dve.reciprocal(wsum[:, :], wsum[:, :]))
                        chain(dve.tensor_scalar(gate[:, :], gate[:, :], wsum[:, :], SCALING * N_SCALE, ALU.mult, ALU.mult))
                        if fleast(i) >= 1:
                            dve.wait_ge(hw_turned, i)
                        chain(dve.tensor_tensor(hw[:, :].rearrange("p (e r) -> p e r", e=E),
                                                logit[:, 0:E * R].rearrange("p (e r) -> p e r", e=E),
                                                gate[:, :].rearrange("p (e r) -> p e r", r=1).to_broadcast([128, E, R]),
                                                ALU.mult))

                    def hw_lo(i):
                        if fleast(i) >= 1:
                            dve.wait_ge(dense_made, 4 * i)
                        dve.wait_ge(hwt_hi_made, i + 1)
                        dve.tensor_tensor(hwt_lo[:, :], hw_bank[:, 0:128], hwt_hi[:, :], ALU.subtract).then_inc(hwt_lo_made, 1)

                    def finish(i, par):
                        dve.wait_ge(bias_added, i + 1)
                        for o in range(4):
                            cols = slice(o * 512, (o + 1) * 512)
                            dve.wait_ge(dense_made, 4 * i + o + 1)
                            dve.scalar_tensor_tensor(out=row[:, par, cols], in0=dense[o][:, :], scalar=out_gate[:, :],
                                                     in1=row[:, par, cols], op0=ALU.mult, op1=ALU.add).then_inc(out_ready, 1)

                    def step(i, par):
                        gating(i)
                        if fmost(i) + 1 < ROWS:
                            dve.wait_ge(x2_loaded[1 - par], 16 * ((i + 1) // 2 + 1))
                            dve.nop(nofuse=True)
                            statistics(i + 1, row[:, 1 - par, :])
                        hw_lo(i)
                        if fmost(i) + 1 < ROWS:
                            turned_lo(i + 1, 0, 2)
                        finish(i, par)
                        if fmost(i) + 1 < ROWS:
                            turned_lo(i + 1, 2, 4)

                    weights_lo(0, 4 * EARLY)
                    dve.wait_ge(first_loaded, 16)
                    statistics(0, norm)
                    weights_lo(4 * EARLY, 4 * JOBS)
                    dve.wait_ge(small_loaded, 32)
                    dve.tensor_scalar(bias[:, :], bias[:, :], gates[:, 1:2], None, ALU.mult).then_inc(bias_ready, 1)
                    dve.tensor_scalar(out_gate[:, :], gates[:, 1:2], DESCALE, None, ALU.mult).then_inc(bias_ready, 1)
                    dve.tensor_scalar(thr_b[:, :], thr_b[:, :], -1.0, None, ALU.mult).then_inc(bias_ready, 1)
                    turned_lo(0, 0, 4)
                    tiles(dve, step)

                @block.gpsimd
                def _(pool):
                    def step(i, par):
                        if fmost(i) == 0:
                            pool.wait_ge(x2_loaded[0], 16)
                        pool.wait_ge(normed, i + 1)
                        pool.tensor_tensor(row[:, par, :], row[:, par, :], bias[:, :], ALU.add).then_inc(bias_added, 1)

                    pool.wait_ge(bias_ready, 3)
                    tiles(pool, step)


_INS = ['x', 'ctx_4096', 'g_xattn', 'g_ffn', 'L0_ffn_W_base', 'L0_ffn_b_base', 'L0_ffn_W_gate', 'L0_ffn_W_thr',
        'L0_ffn_b_thr', 'L0_ffn_A_w', 'L0_ffn_B_w']


def kernel(**inputs):
    import concourse.bacc as _bacc
    from concourse.bass_utils import run_bass_kernel_spmd as _run

    nc = _bacc.Bacc("TRN2", target_bir_lowering=False, num_devices=1)
    arrays, args = {}, []
    for name, a in [(n, inputs[n]) for n in _INS] + list(zip(("tables", "tables16"), dft_tables())):
        a = np.ascontiguousarray(a)
        arrays[f"in_{name}_dram"] = a
        args.append(nc.dram_tensor(f"in_{name}_dram", a.shape, mybir.dt.from_np(a.dtype), kind="ExternalInput").ap())
    out = nc.dram_tensor("out_0_dram", (B, L, D), mybir.dt.float32, kind="ExternalOutput").ap()
    flamingo_kernel(nc, *args, out)
    r = _run(nc, [arrays], core_ids=[0])
    return r.results[0]["out_0_dram"]
```
